# Optimizing a Trainium2 kernel written in Bass

```python
import numpy as np
import jax
import jax.numpy as jnp

def _softmax(x, axis=-1):
    return jax.nn.softmax(x, axis=axis)

def _gelu(x):
    return jax.nn.gelu(x, approximate=True)

def _silu(x):
    return jax.nn.silu(x)

def _sigmoid(x):
    return jax.nn.sigmoid(x)

def _layernorm(x, axis=-1, eps=1e-05):
    m = jnp.mean(x, axis=axis, keepdims=True)
    v = jnp.var(x, axis=axis, keepdims=True)
    return (x - m) / jnp.sqrt(v + eps)

def _scatter_add(tgt, idx, src, axis=0):
    return tgt.at[idx].add(src)

def _segment_sum(src, seg, n):
    return jax.ops.segment_sum(src, seg, n)
kernel_name = 'mk_adaln_d1_jaxref_r8_904135'

def setup_inputs(seed: int=0):
    np.random.seed(seed)
    _w = jnp.asarray

    def _L0_attn_setup():
        import jax, jax.numpy as jnp
        import numpy as np
        B, S = (2, 256)
        HIDDEN, MLP = (128, 256)
        N_STATE, DT_RANK, CONV_K = (16, 64, 4)

        def _causal_depthwise_conv(u, conv_w, conv_b):
            u_pad = jnp.pad(u, ((0, 0), (CONV_K - 1, 0), (0, 0)))
            seq = u.shape[1]
            y = sum((u_pad[:, k:k + seq, :] * conv_w[:, k] for k in range(CONV_K)))
            return y + conv_b

        def _selective_scan(u, A_log, x_proj_w, dt_proj_w, dt_proj_b, D_skip):
            xp = u @ x_proj_w
            delta = jax.nn.softplus(xp[..., :DT_RANK] @ dt_proj_w + dt_proj_b)
            Bm = xp[..., DT_RANK:DT_RANK + N_STATE]
            Cm = xp[..., DT_RANK + N_STATE:]
            A = -jnp.exp(A_log)
            dA = jnp.exp(delta[..., None] * A)
            dBu = delta[..., None] * Bm[:, :, None, :] * u[..., None]

            def step(h, inp):
                dA_t, dBu_t, C_t = inp
                h = dA_t * h + dBu_t
                y = jnp.einsum('bdn,bn->bd', h, C_t)
                return (h, y)
            h0 = jnp.zeros((u.shape[0], u.shape[2], N_STATE), u.dtype)
            _, ys = jax.lax.scan(step, h0, (dA.transpose(1, 0, 2, 3), dBu.transpose(1, 0, 2, 3), Cm.transpose(1, 0, 2)))
            return ys.transpose(1, 0, 2) + u * D_skip
        key = jax.random.key(seed)
        ks = jax.random.split(key, 14)
        s = 0.02
        return {'x': jax.random.normal(ks[0], (B, S, HIDDEN), jnp.float32), 'W1': jax.random.normal(ks[1], (HIDDEN, MLP), jnp.float32) * s, 'b1': jnp.zeros((MLP,), jnp.float32), 'W2': jax.random.normal(ks[2], (HIDDEN, MLP), jnp.float32) * s, 'b2': jnp.zeros((MLP,), jnp.float32), 'conv_w': jax.random.normal(ks[3], (MLP, CONV_K), jnp.float32) * s, 'conv_b': jnp.zeros((MLP,), jnp.float32), 'A_log': jnp.log(jnp.broadcast_to(jnp.arange(1, N_STATE + 1, dtype=jnp.float32), (MLP, N_STATE))), 'x_proj_w': jax.random.normal(ks[4], (MLP, DT_RANK + 2 * N_STATE), jnp.float32) * s, 'dt_proj_w': jax.random.normal(ks[5], (DT_RANK, MLP), jnp.float32) * s, 'dt_proj_b': jnp.full((MLP,), -4.0, jnp.float32), 'D_skip': jnp.ones((MLP,), jnp.float32), 'Wo': jax.random.normal(ks[6], (MLP, HIDDEN), jnp.float32) * s, 'bo': jnp.zeros((HIDDEN,), jnp.float32)}
    _L0_attn_in = _L0_attn_setup()

    def _L0_ffn_setup():
        import jax, jax.numpy as jnp
        import numpy as np
        H = 128
        I = 352
        E = 8
        TOP_K = 2

        def _moe(hidden_states, router_w, gate_w, up_w, down_w):
            B, S, Hd = hidden_states.shape
            x = hidden_states.reshape(-1, Hd)
            logits = x @ router_w.T
            probs = jax.nn.softmax(logits.astype(jnp.float32), axis=-1)
            top_w, top_idx = jax.lax.top_k(probs, TOP_K)
            top_w = top_w.astype(x.dtype)
            onehot = jax.nn.one_hot(top_idx, E, dtype=x.dtype)
            w_te = jnp.einsum('tk,tke->te', top_w, onehot)
            g = jnp.einsum('th,eih->tei', x, gate_w)
            u = jnp.einsum('th,eih->tei', x, up_w)
            h = jax.nn.silu(g) * u
            y = jnp.einsum('tei,ehi,te->th', h, down_w, w_te)
            return y.reshape(B, S, Hd)
        key = jax.random.key(seed)
        ks = jax.random.split(key, 5)
        s = 0.02
        return {'hidden_states': jax.random.normal(ks[0], (2, 128, H), dtype=jnp.float32), 'router_w': jax.random.normal(ks[1], (E, H), dtype=jnp.float32) * s, 'gate_w': jax.random.normal(ks[2], (E, I, H), dtype=jnp.float32) * s, 'up_w': jax.random.normal(ks[3], (E, I, H), dtype=jnp.float32) * s, 'down_w': jax.random.normal(ks[4], (E, H, I), dtype=jnp.float32) * s}
    _L0_ffn_in = _L0_ffn_setup()
    _L0_c = _w((lambda *s: np.random.randn(*s).astype(np.float32) * 0.05)(4, 128))
    _L0_wmod = _w((lambda *s: np.random.randn(*s).astype(np.float32) * 0.05)(128, 6 * 128) * 128 ** (-0.5))
    _d = {'L0_attn_x': _L0_attn_in['x'], 'L0_attn_W1': _L0_attn_in['W1'], 'L0_attn_b1': _L0_attn_in['b1'], 'L0_attn_W2': _L0_attn_in['W2'], 'L0_attn_b2': _L0_attn_in['b2'], 'L0_attn_conv_w': _L0_attn_in['conv_w'], 'L0_attn_conv_b': _L0_attn_in['conv_b'], 'L0_attn_A_log': _L0_attn_in['A_log'], 'L0_attn_x_proj_w': _L0_attn_in['x_proj_w'], 'L0_attn_dt_proj_w': _L0_attn_in['dt_proj_w'], 'L0_attn_dt_proj_b': _L0_attn_in['dt_proj_b'], 'L0_attn_D_skip': _L0_attn_in['D_skip'], 'L0_attn_Wo': _L0_attn_in['Wo'], 'L0_attn_bo': _L0_attn_in['bo'], 'L0_ffn_router_w': _L0_ffn_in['router_w'], 'L0_ffn_gate_w': _L0_ffn_in['gate_w'], 'L0_ffn_up_w': _L0_ffn_in['up_w'], 'L0_ffn_down_w': _L0_ffn_in['down_w'], 'L0_c': _L0_c, 'L0_wmod': _L0_wmod}
    _x0 = _d['L0_attn_x']
    _d['L0_attn_x'] = jax.random.normal(jax.random.fold_in(jax.random.key(seed), 1), (4, 1024, 128), dtype=_x0.dtype)
    del _x0
    return _d

def reference(L0_attn_x, L0_attn_W1, L0_attn_b1, L0_attn_W2, L0_attn_b2, L0_attn_conv_w, L0_attn_conv_b, L0_attn_A_log, L0_attn_x_proj_w, L0_attn_dt_proj_w, L0_attn_dt_proj_b, L0_attn_D_skip, L0_attn_Wo, L0_attn_bo, L0_ffn_router_w, L0_ffn_gate_w, L0_ffn_up_w, L0_ffn_down_w, L0_c, L0_wmod):

    def _L0_attn_ref(x, W1, b1, W2, b2, conv_w, conv_b, A_log, x_proj_w, dt_proj_w, dt_proj_b, D_skip, Wo, bo):
        import jax, jax.numpy as jnp
        import numpy as np
        B, S = (2, 256)
        HIDDEN, MLP = (128, 256)
        N_STATE, DT_RANK, CONV_K = (16, 64, 4)

        def _causal_depthwise_conv(u, conv_w, conv_b):
            u_pad = jnp.pad(u, ((0, 0), (CONV_K - 1, 0), (0, 0)))
            seq = u.shape[1]
            y = sum((u_pad[:, k:k + seq, :] * conv_w[:, k] for k in range(CONV_K)))
            return y + conv_b

        def _selective_scan(u, A_log, x_proj_w, dt_proj_w, dt_proj_b, D_skip):
            xp = u @ x_proj_w
            delta = jax.nn.softplus(xp[..., :DT_RANK] @ dt_proj_w + dt_proj_b)
            Bm = xp[..., DT_RANK:DT_RANK + N_STATE]
            Cm = xp[..., DT_RANK + N_STATE:]
            A = -jnp.exp(A_log)
            dA = jnp.exp(delta[..., None] * A)
            dBu = delta[..., None] * Bm[:, :, None, :] * u[..., None]

            def step(h, inp):
                dA_t, dBu_t, C_t = inp
                h = dA_t * h + dBu_t
                y = jnp.einsum('bdn,bn->bd', h, C_t)
                return (h, y)
            h0 = jnp.zeros((u.shape[0], u.shape[2], N_STATE), u.dtype)
            _, ys = jax.lax.scan(step, h0, (dA.transpose(1, 0, 2, 3), dBu.transpose(1, 0, 2, 3), Cm.transpose(1, 0, 2)))
            return ys.transpose(1, 0, 2) + u * D_skip
        gate = jax.nn.sigmoid(x @ W2 + b2)
        u = x @ W1 + b1
        u = jax.nn.sigmoid(_causal_depthwise_conv(u, conv_w, conv_b))
        y = _selective_scan(u, A_log, x_proj_w, dt_proj_w, dt_proj_b, D_skip)
        return y * gate @ Wo + bo

    def _L0_ffn_ref(hidden_states, router_w, gate_w, up_w, down_w):
        import jax, jax.numpy as jnp
        import numpy as np
        H = 128
        I = 352
        E = 8
        TOP_K = 2

        def _moe(hidden_states, router_w, gate_w, up_w, down_w):
            B, S, Hd = hidden_states.shape
            x = hidden_states.reshape(-1, Hd)
            logits = x @ router_w.T
            probs = jax.nn.softmax(logits.astype(jnp.float32), axis=-1)
            top_w, top_idx = jax.lax.top_k(probs, TOP_K)
            top_w = top_w.astype(x.dtype)
            onehot = jax.nn.one_hot(top_idx, E, dtype=x.dtype)
            w_te = jnp.einsum('tk,tke->te', top_w, onehot)
            g = jnp.einsum('th,eih->tei', x, gate_w)
            u = jnp.einsum('th,eih->tei', x, up_w)
            h = jax.nn.silu(g) * u
            y = jnp.einsum('tei,ehi,te->th', h, down_w, w_te)
            return y.reshape(B, S, Hd)
        return _moe(hidden_states, router_w, gate_w, up_w, down_w)
    x = L0_attn_x
    mod = (_silu(L0_c) @ L0_wmod).reshape(L0_c.shape[0], 6, 1, -1)
    sa, ca, ga, sb, cb, gb = (mod[:, 0], mod[:, 1], mod[:, 2], mod[:, 3], mod[:, 4], mod[:, 5])
    ga = (2 * (ga >= 0) - 1) * jnp.maximum(jnp.abs(ga), 0.25)
    gb = (2 * (gb >= 0) - 1) * jnp.maximum(jnp.abs(gb), 0.25)
    h = _layernorm(x, axis=-1) * (1 + ca) + sa
    x = x + ga * _L0_attn_ref(h, L0_attn_W1, L0_attn_b1, L0_attn_W2, L0_attn_b2, L0_attn_conv_w, L0_attn_conv_b, L0_attn_A_log, L0_attn_x_proj_w, L0_attn_dt_proj_w, L0_attn_dt_proj_b, L0_attn_D_skip, L0_attn_Wo, L0_attn_bo)
    h = _layernorm(x, axis=-1) * (1 + cb) + sb
    x = x + gb * _L0_ffn_ref(h, L0_ffn_router_w, L0_ffn_gate_w, L0_ffn_up_w, L0_ffn_down_w)
    return x

_drawn_inputs = setup_inputs


def setup_inputs(seed=0):
    import zlib

    import numpy as np

    out = dict(_drawn_inputs(seed))
    spreads = {'L0_attn_b1': (0.0, 0.8),
     'L0_attn_b2': (0.0, 0.8),
     'L0_attn_conv_b': (0.0, 0.8),
     'L0_attn_dt_proj_b': (-4.0, 0.6),
     'L0_attn_D_skip': (1.0, 0.6),
     'L0_attn_bo': (0.0, 0.324)}
    factors = {'L0_attn_W1': 8.0,
     'L0_attn_W2': 8.0,
     'L0_attn_conv_w': 8.0,
     'L0_attn_A_log': 8.0,
     'L0_attn_x_proj_w': 8.0,
     'L0_attn_dt_proj_w': 8.0,
     'L0_attn_Wo': 2.705,
     'L0_ffn_router_w': 8.0,
     'L0_ffn_gate_w': 8.0,
     'L0_ffn_up_w': 8.0,
     'L0_ffn_down_w': 8.0}
    for name, (base, spread) in spreads.items():
        noise = np.random.default_rng([zlib.crc32(name.encode()), seed]).standard_normal(out[name].shape)
        drawn = base * np.exp(spread * noise) if base else spread * noise
        out[name] = jnp.asarray(drawn.astype(out[name].dtype))
    for name, factor in factors.items():
        out[name] = (out[name] * factor).astype(out[name].dtype)
    return out
```

```python
from contextlib import ExitStack

import concourse.bass as bass
from concourse import mybir

fp32 = mybir.dt.float32
ALU = mybir.AluOpType
ACT = mybir.ActivationFunctionType
ds = bass.ds

P = 128
BATCH, SEQ, HID = 4, 1024, 128
MLP, NSTATE, DTRANK, CONVK = 256, 16, 64, 4
EXPERTS, INTER = 8, 352
NTOK = BATCH * SEQ
HALVES = MLP // P
BANK = 512
CH = SEQ // P
SEG = SEQ // BANK
LN_EPS = 1e-5
NORMS = 2
PROJ = DTRANK + 2 * NSTATE
TILE = 512
NTILE = NTOK // TILE
TCH = TILE // P
INNER = [(c * P, min(P, INTER - c * P)) for c in range(-(-INTER // P))]
NIN = len(INNER)
STEPS = EXPERTS * NIN
MOD_STEPS = 11
PRIMED = 1
DA_SLOTS, SCAN_SLOTS, C_SLOTS = 4, 3, 2

FILLS = (["mean0", "rstd0", "u0", "u1", "gate0", "gate1", "xdt", "dt0", "dt1"]
         + [f"C{n}" for n in range(NSTATE)] + ["yT0", "yT1", "mean1", "rstd1"])
FILL_NO = {name: i for i, name in enumerate(FILLS)}


def adaln_kernel(nc, xT_d, w1_d, w2_d, wo_d, xproj_d, dtw_d, alog_d, conv_d, cols_d, bo_d, router_d,
                 gate_d, up_d, down_d, cT_d, wmod_d, outT_d):
    ctx = ExitStack()
    with ctx:
        def sb(name, shape):
            return ctx.enter_context(nc.sbuf_tensor(name, shape, fp32))

        def sem(name):
            return ctx.enter_context(nc.semaphore(name))

        xT = sb("xT", [P, NTOK])
        h2T = sb("h2T", [P, NTOK])
        ident = sb("ident", [P, P])
        mean_w = sb("mean_w", [P, P])
        w1 = sb("w1", [P, MLP])
        w2 = sb("w2", [P, MLP])
        wo = sb("wo", [P, HALVES, HID])
        xproj = sb("xproj", [P, HALVES, PROJ])
        dtw = sb("dtw", [DTRANK, MLP])
        A = sb("A", [P, HALVES, NSTATE])
        conv = sb("conv", [P, HALVES, CONVK])
        cols = sb("cols", [P, 5, HALVES])
        bo = sb("bo", [P, 1])
        Ddiag = sb("Ddiag", [P, HALVES, P])
        router = sb("router", [P, EXPERTS])
        gate_w = sb("gate_w", [P, EXPERTS, INTER])
        up_w = sb("up_w", [P, EXPERTS, INTER])
        cT = sb("cT", [P, BATCH])
        siluc = sb("siluc", [P, BATCH])
        wmod = sb("wmod", [P, 6, P])
        mod = sb("mod", [P, 6, BATCH])
        modt = sb("modt", [P, 2, BATCH])
        gabo = sb("gabo", [P, BATCH])
        gb8 = sb("gb8", [P, NTILE])
        xc = sb("xc", [P, SEQ])
        hT = sb("hT", [P, SEQ])
        u = sb("u", [P, HALVES, SEQ])
        gate = sb("gate", [P, HALVES, SEQ])
        xdt = sb("xdt", [DTRANK, SEQ])
        delta = sb("delta", [P, HALVES, SEQ])
        du = sb("du", [P, HALVES, SEQ])
        bcT = sb("bcT", [P, CH, 2 * NSTATE])
        ta = sb("ta", [P, HALVES * SEQ + 2 * P])
        tb = sb("tb", [P, HALVES, SEQ])
        tc = sb("tc", [P, HALVES, SEQ])
        td = sb("td", [P, HALVES, SEQ])
        Csb = sb("Csb", [P, C_SLOTS, SEQ])
        dA = sb("dA", [P, DA_SLOTS, SEQ])
        ring = sb("ring", [P, SCAN_SLOTS, HALVES, SEQ])
        small = sb("small", [P, 6, CH])
        logits = sb("logits", [P, BATCH, CH, EXPERTS])

        lg = logits[:, :, :, :].rearrange("p b c e -> p (b c) e")
        ta2 = ta[:, 0:HALVES * SEQ].rearrange("p (a s) -> p a s", a=HALVES)
        PAD = SEQ + P
        ub = ta[:, :].rearrange("p (a s) -> p a s", a=HALVES)[:, :, P - CONVK + 1:PAD]
        ubpad = ta[:, :].rearrange("p (a s) -> p a s", a=HALVES)[:, :, P - CONVK + 1:P]

        psum = ctx.enter_context(nc.psum_tensor("psum", [P, 8 * BANK], fp32))
        PY = psum[:, 0:4 * BANK]
        PYc = PY.rearrange("p (c m) -> p c m", c=CH)
        PB = psum[:, 4 * BANK:6 * BANK]
        PF = psum[:, 6 * BANK:8 * BANK]
        PS = psum[:, 0:BANK]

        ysb = ta[:, 0:CH * MLP].rearrange("p (c m) -> p c m", c=CH)

        down_w = ring[:, :, :, :].rearrange("p r a s -> p (r a s)")[:, 0:STEPS * HID].rearrange(
            "p (e c h) -> p e c h", e=EXPERTS, c=NIN)
        wte = sb("wte", [P, BATCH * CH, EXPERTS])
        wt = sb("wt", [P, TCH, EXPERTS])
        before = sb("before", [P, EXPERTS, EXPERTS])
        stat = sb("stat", [P, 2, BATCH * CH])
        xw = u[:, :, 0:TILE]
        silu = gate[:, :, 0:TILE]
        inner = delta[:, :, 0:TILE]
        moe = xc[:, 0:TILE]

        def bank(i):
            return psum[:, i * BANK:(i + 1) * BANK]

        def PG(s):
            return bank(s % 2)

        def PU(s):
            return bank(2 + s % 2)

        def PW(e):
            return bank(4 + e % 2)

        PO = bank(6)

        load = {n: sem(f"load_{n}") for n in ("x", "c", "attn", "moe", "down")}
        ident_zero = sem("ident_zero")
        ident_ready = sem("ident_ready")
        const_ready = sem("const_ready")
        siluc_ready = sem("siluc_ready")
        mod_filled = sem("mod_filled")
        mod_step = sem("mod_step")
        a_exp = sem("a_exp")
        a_ready = sem("a_ready")
        fill = sem("fill")
        drained = sem("drained")
        sq_ready = sem("sq_ready")
        var_ready = sem("var_ready")
        v_ready = sem("v_ready")
        lnv_ready = sem("lnv_ready")
        y0_ready = sem("y0_ready")
        newton = sem("newton")
        rstd_ready = sem("rstd_ready")
        h_ready = sem("h_ready")
        h2_ready = sem("h2_ready")
        ub_ready = sem("ub_ready")
        conv_step = sem("conv_step")
        u_ready = sem("u_ready")
        bc_filled = sem("bc_filled")
        bc_ready = sem("bc_ready")
        av_ready = sem("av_ready")
        e_ready = sem("e_ready")
        lw_ready = sem("lw_ready")
        sp_step = sem("sp_step")
        delta_ready = sem("delta_ready")
        du_ready = sem("du_ready")
        b_filled = sem("b_filled")
        dbu_ready = sem("dbu_ready")
        da_ready = sem("da_ready")
        scanned = sem("scanned")
        prod_ready = sem("prod_ready")
        summed = sem("summed")
        d_added = sem("d_added")
        y_out = sem("y_out")
        o_filled = sem("o_filled")
        o_ready = sem("o_ready")
        x1_ready = sem("x1_ready")
        logit_filled = sem("logit_filled")
        logit_ready = sem("logit_ready")
        top_step = sem("top_step")
        lexp = sem("lexp")
        wt_ready = sem("wt_ready")
        wb_filled = sem("wb_filled")
        xw_ready = sem("xw_ready")
        g_filled = sem("g_filled")
        up_filled = sem("up_filled")
        silu_ready = sem("silu_ready")
        inner_ready = sem("inner_ready")
        down_done = sem("down_done")
        moe_filled = sem("moe_filled")
        moe_scaled = sem("moe_scaled")
        out_ready = sem("out_ready")
        stored = sem("stored")

        def scan_slot(n):
            return n % SCAN_SLOTS

        def fill_no(b, name):
            return b * len(FILLS) + FILL_NO[name]

        primed = [logit_ready, drained, h2_ready, x1_ready, dbu_ready, summed, prod_ready, scanned, wb_filled, silu_ready, inner_ready, xw_ready, moe_scaled, down_done]
        block = ctx.enter_context(nc.Block())

        @block.sync
        def _(sp):
            sp.dma_start(cT[:, :], cT_d).then_inc(load["c"], 16)
            sp.dma_start(wmod[:, :, :], wmod_d.rearrange("h (k m) -> h k m", k=6)).then_inc(load["c"], 16)
            sp.dma_start(bo[:, :], bo_d).then_inc(load["c"], 16)
            sp.dma_start(xT[:, :], xT_d).then_inc(load["x"], 16)
            sp.dma_start(w1[:, :], w1_d).then_inc(load["attn"], 16)
            sp.dma_start(w2[:, :], w2_d).then_inc(load["attn"], 16)
            sp.dma_start(wo[:, :, :], wo_d.rearrange("(a p) m -> p a m", p=P)).then_inc(load["attn"], 16)
            sp.dma_start(xproj[:, :, :], xproj_d.rearrange("(a p) m -> p a m", p=P)).then_inc(load["attn"], 16)
            sp.dma_start(dtw[:, :], dtw_d).then_inc(load["attn"], 16)
            sp.dma_start(A[:, :, :], alog_d.rearrange("(a p) m -> p a m", p=P)).then_inc(load["attn"], 16)
            sp.dma_start(conv[:, :, :], conv_d.rearrange("(a p) m -> p a m", p=P)).then_inc(load["attn"], 16)
            sp.dma_start(cols[:, :, :], cols_d.rearrange("p (k a) -> p k a", k=5)).then_inc(load["attn"], 16)
            sp.dma_start(router[:, :], router_d).then_inc(load["attn"], 16)
            sp.dma_start(gate_w[:, :, :], gate_d.rearrange("h (e i) -> h e i", e=EXPERTS)).then_inc(load["moe"], 16)
            sp.dma_start(up_w[:, :, :], up_d.rearrange("h (e i) -> h e i", e=EXPERTS)).then_inc(load["moe"], 16)
            sp.wait_ge(summed, PRIMED + BATCH * NSTATE)
            for c, (i0, k) in enumerate(INNER):
                sp.dma_start(down_w[0:k, :, c, :],
                             down_d.rearrange("(e i) h -> i e h", e=EXPERTS)[i0:i0 + k, :, :]).then_inc(load["down"], 16)
            with sp.Fori(0, NTILE) as j:
                sp.wait_ge(out_ready, j + 1)
                sp.dma_start(outT_d[:, ds(j * TILE, TILE)], xT[:, ds(j * TILE, TILE)]).then_inc(stored, 16)
            sp.wait_ge(stored, 16 * NTILE)

        @block.gpsimd
        def _(pool):
            for signal in primed:
                pool.sem_inc(signal, PRIMED)
            nc.gpsimd.memset(ident[:, :], 0.0).then_inc(ident_zero, 1)
            pool.wait_ge(ident_zero, 1)
            nc.gpsimd.affine_select(out=ident[:, :], in_=ident[:, :], compare_op=ALU.not_equal, fill=1.0, base=0,
                                    pattern=[[-1, P]], channel_multiplier=1).then_inc(ident_ready, 1)
            nc.gpsimd.memset(before[:, :, :], 1.0).then_inc(ident_zero, 1)
            pool.wait_ge(ident_zero, 2)
            nc.gpsimd.affine_select(out=before[:, :, :], in_=before[:, :, :], compare_op=ALU.is_gt, fill=0.0, base=0,
                                    pattern=[[1, EXPERTS], [-1, EXPERTS]], channel_multiplier=0).then_inc(ident_ready, 1)
            with pool.Fori(0, BATCH) as b:
                for n in range(NSTATE):
                    step = b * NSTATE + n
                    s = scan_slot(n)
                    pool.wait_ge(scanned, PRIMED + (step + 1) * HALVES)
                    pool.wait_ge(drained, PRIMED + fill_no(b, f"C{n}") + 1)
                    nc.gpsimd.tensor_tensor(ring[:, s], ring[:, s],
                                            Csb[:, n % C_SLOTS, :].unsqueeze(1).to_broadcast([P, HALVES, SEQ]),
                                            ALU.mult).then_inc(prod_ready, 1)

        @block.tensor
        def _(pe):
            def product(out, lhsT, rhs, start=True, stop=True):
                return nc.tensor.matmul(out, lhsT, rhs, start=start, stop=stop)

            def spread(out, column, first=True):
                return nc.tensor.matmul(out, column.to_broadcast([P, P]), ident[:, :], is_transpose=True,
                                        start=first, stop=True, skip_group_check=True)

            def room(b, name):
                pe.wait_ge(drained, PRIMED + fill_no(b, name))

            def norm(b, k, first_wait):
                first_wait()
                room(b, f"mean{k}")
                for g in range(SEG):
                    last = product(PF[:, g * BANK:(g + 1) * BANK], mean_w[:, :], xT[:, ds(b * SEQ + g * BANK, BANK)])
                last.then_inc(fill, 1)
                pe.wait_ge(sq_ready, b * NORMS + k + 1)
                for c in range(CH):
                    last = product(PS[:, c:c + 1], td[:, 0, c * P:(c + 1) * P], mean_w[:, 0:1])
                last.then_inc(var_ready, 1)
                pe.wait_ge(rstd_ready, b * NORMS + k + 1)
                room(b, f"rstd{k}")
                for c in range(CH):
                    last = spread(PF[:, c * P:(c + 1) * P], small[:, 5, c:c + 1])
                last.then_inc(fill, 1)

            pe.wait_ge(load["c"], 48)
            pe.wait_ge(siluc_ready, 1)
            for k in range(6):
                last = product(PB[:, k * BATCH:(k + 1) * BATCH], wmod[:, k, :], siluc[:, :])
            last.then_inc(mod_filled, 1)
            pe.wait_ge(ident_ready, 1)
            pe.wait_ge(const_ready, 1)
            pe.wait_ge(load["x"], 16)
            pe.wait_ge(load["attn"], 16 * 9)
            pe.wait_ge(mod_step, MOD_STEPS)
            with pe.Fori(0, BATCH) as b:
                def y_bank_free():
                    pe.wait_ge(logit_ready, PRIMED + b)
                norm(b, 0, y_bank_free)
                pe.wait_ge(h_ready, b * NORMS + 1)
                for w, name in ((w1, "u"), (w2, "gate")):
                    for a in range(HALVES):
                        room(b, f"{name}{a}")
                        for g in range(SEG):
                            last = product(PF[:, g * BANK:(g + 1) * BANK], w[:, a * P:(a + 1) * P],
                                           hT[:, g * BANK:(g + 1) * BANK])
                        last.then_inc(fill, 1)
                pe.wait_ge(u_ready, b + 1)
                room(b, "xdt")
                for g in range(SEG):
                    for a in range(HALVES):
                        last = product(PF[0:DTRANK, g * BANK:(g + 1) * BANK], xproj[:, a, 0:DTRANK],
                                       u[:, a, g * BANK:(g + 1) * BANK], a == 0, a == HALVES - 1)
                last.then_inc(fill, 1)
                for c in range(CH):
                    for a in range(HALVES):
                        last = product(PS[:, c * 2 * NSTATE:(c + 1) * 2 * NSTATE], u[:, a, c * P:(c + 1) * P],
                                       xproj[:, a, DTRANK:PROJ], a == 0, a == HALVES - 1)
                last.then_inc(bc_filled, 1)
                pe.wait_ge(drained, PRIMED + fill_no(b, "xdt") + 1)
                for a in range(HALVES):
                    room(b, f"dt{a}")
                    for g in range(SEG):
                        last = product(PF[:, g * BANK:(g + 1) * BANK], dtw[:, a * P:(a + 1) * P],
                                       xdt[:, g * BANK:(g + 1) * BANK])
                    last.then_inc(fill, 1)
                pe.wait_ge(bc_ready, b + 1)
                for c in range(CH):
                    for a in range(HALVES):
                        last = nc.tensor.matmul(PYc[:, c, a * P:(a + 1) * P], u[:, a, c * P:(c + 1) * P], Ddiag[:, a, :],
                                                start=(c % 2 == 0 and a == 0), stop=True, skip_group_check=True)
                last.then_inc(d_added, 1)

                def add_state(n):
                    s = scan_slot(n)
                    pe.wait_ge(prod_ready, PRIMED + b * NSTATE + n + 1)
                    for c in range(CH):
                        for a in range(HALVES):
                            last = nc.tensor.matmul(PYc[:, c, a * P:(a + 1) * P], ring[:, s, a, c * P:(c + 1) * P],
                                                    ident[:, :], is_transpose=True, start=False, stop=True,
                                                    skip_group_check=True)
                    last.then_inc(summed, 1)

                for n in range(NSTATE):
                    pe.wait_ge(dbu_ready, PRIMED + b * NSTATE + n)
                    for c in range(CH):
                        last = spread(PB[:, c * P:(c + 1) * P], bcT[:, c, n:n + 1])
                    last.then_inc(b_filled, 1)
                    room(b, f"C{n}")
                    for c in range(CH):
                        last = spread(PF[:, c * P:(c + 1) * P], bcT[:, c, NSTATE + n:NSTATE + n + 1])
                    last.then_inc(fill, 1)
                    if n >= 2:
                        add_state(n - 2)
                add_state(NSTATE - 2)
                add_state(NSTATE - 1)
                pe.wait_ge(y_out, b + 1)
                for a in range(HALVES):
                    room(b, f"yT{a}")
                    for c in range(CH):
                        last = nc.tensor.matmul(PF[:, c * P:(c + 1) * P],
                                                ysb[:, c, a * P:(a + 1) * P], ident[:, :], is_transpose=True,
                                                start=True, stop=True, skip_group_check=True)
                    last.then_inc(fill, 1)
                pe.wait_ge(drained, PRIMED + fill_no(b, "yT1") + 1)
                for g in range(SEG):
                    for a in range(HALVES):
                        last = product(PB[:, g * BANK:(g + 1) * BANK], wo[:, a, :], tb[:, a, g * BANK:(g + 1) * BANK],
                                       a == 0, a == HALVES - 1)
                last.then_inc(o_filled, 1)
                norm(b, 1, lambda: pe.wait_ge(x1_ready, PRIMED + b + 1))
                pe.wait_ge(h_ready, b * NORMS + 2)
                for c in range(CH):
                    last = product(PS[:, c * EXPERTS:(c + 1) * EXPERTS], hT[:, c * P:(c + 1) * P], router[:, :])
                last.then_inc(logit_filled, 1)

            pe.wait_ge(load["moe"], 32)
            pe.wait_ge(load["down"], 16 * NIN)
            pe.wait_ge(h2_ready, PRIMED + BATCH)
            pe.wait_ge(o_ready, BATCH)
            pe.wait_ge(logit_ready, PRIMED + BATCH)
            pe.wait_ge(drained, PRIMED + BATCH * len(FILLS))
            with pe.Fori(0, NTILE) as j:
                pe.wait_ge(wt_ready, j + 1)

                def weigh(e):
                    if e >= 2:
                        pe.wait_ge(xw_ready, PRIMED + j * EXPERTS + e - 1)
                    else:
                        pe.wait_ge(xw_ready, PRIMED + j * EXPERTS)
                    for c in range(TCH):
                        last = spread(PW(e)[:, c * P:(c + 1) * P], wt[:, c, e:e + 1])
                    last.then_inc(wb_filled, 1)

                def down(s):
                    e, c = divmod(s, NIN)
                    k = INNER[c][1]
                    pe.wait_ge(inner_ready, PRIMED + j * STEPS + s + 1)
                    last = product(PO, down_w[0:k, e, c, :], inner[0:k, s % 2, :], s == 0, s == STEPS - 1)
                    last.then_inc(down_done, 1)
    
                weigh(0)
                for e in range(EXPERTS):
                    if e + 1 < EXPERTS:
                        weigh(e + 1)
                    for c, (i0, k) in enumerate(INNER):
                        s = e * NIN + c
                        pe.wait_ge(silu_ready, PRIMED + j * STEPS + max(s - 1, 0))
                        product(PG(s)[0:k, :], gate_w[:, e, i0:i0 + k], h2T[:, ds(j * TILE, TILE)]).then_inc(g_filled, 1)
                        if c == 0:
                            pe.wait_ge(xw_ready, PRIMED + j * EXPERTS + e + 1)
                        pe.wait_ge(inner_ready, PRIMED + j * STEPS + max(s - 1, 0))
                        product(PU(s)[0:k, :], up_w[:, e, i0:i0 + k], xw[:, e % 2, :]).then_inc(up_filled, 1)
                        if s == 1:
                            pe.wait_ge(moe_scaled, PRIMED + j)
                        if s >= 1:
                            down(s - 1)
                down(STEPS - 1)

        @block.scalar
        def _(act):
            def norm(b, k):
                i = b * NORMS + k + 1
                act.wait_ge(drained, PRIMED + fill_no(b, f"mean{k}") + 1)
                nc.scalar.activation(td[:, 0, :], xc[:, :], ACT.Square).then_inc(sq_ready, 1)
                act.wait_ge(v_ready, i)
                nc.scalar.activation(small[:, 1, :], small[:, 0, :], ACT.Ln).then_inc(lnv_ready, 1)
                act.wait_ge(lnv_ready, i)
                nc.scalar.activation(small[:, 2, :], small[:, 1, :], ACT.Exp, scale=-0.5).then_inc(y0_ready, 1)
                act.wait_ge(drained, PRIMED + fill_no(b, f"rstd{k}") + 1)
                scale, bias = mod[:, 3 * k + 1, ds(b, 1)], mod[:, 3 * k, ds(b, 1)]
                nc.scalar.activation(hT[:, :], xc[:, :], ACT.Identity, scale=scale, bias=bias).then_inc(h_ready, 1)
                if k == 1:
                    nc.scalar.activation(h2T[:, ds(b * SEQ, SEQ)], xc[:, :], ACT.Identity, scale=scale,
                                         bias=bias).then_inc(h2_ready, 1)

            act.wait_ge(load["c"], 48)
            nc.scalar.activation(siluc[:, :], cT[:, :], ACT.Silu).then_inc(siluc_ready, 1)
            act.wait_ge(load["attn"], 16 * 9)
            nc.scalar.activation(A[:, :, :], A[:, :, :], ACT.Exp).then_inc(a_exp, 1)
            act.wait_ge(mod_step, MOD_STEPS)
            with act.Fori(0, BATCH) as b:
                norm(b, 0)
                act.wait_ge(x1_ready, PRIMED + b)
                for a in range(HALVES):
                    act.wait_ge(fill, fill_no(b, f"u{a}") + 1)
                    nc.scalar.activation(ub[:, a, CONVK - 1:], PF, ACT.Identity, bias=cols[:, 0, a:a + 1]).then_inc(drained, 1)
                for a in range(HALVES):
                    act.wait_ge(fill, fill_no(b, f"gate{a}") + 1)
                    nc.scalar.activation(gate[:, a, :], PF, ACT.Sigmoid, bias=cols[:, 1, a:a + 1]).then_inc(drained, 1)
                act.wait_ge(conv_step, (b + 1) * CONVK * HALVES)
                nc.scalar.activation(u[:, :, :], tb[:, :, :], ACT.Sigmoid).then_inc(u_ready, 1)
                act.wait_ge(fill, fill_no(b, "xdt") + 1)
                nc.scalar.copy(xdt[:, :], PF[0:DTRANK, :]).then_inc(drained, 1)
                for a in range(HALVES):
                    act.wait_ge(fill, fill_no(b, f"dt{a}") + 1)
                    nc.scalar.activation(tc[:, a, :], PF, ACT.Identity, bias=cols[:, 3, a:a + 1]).then_inc(drained, 1)
                act.wait_ge(drained, PRIMED + fill_no(b, "dt1") + 1)
                nc.scalar.activation(ta2, tc[:, :, :], ACT.Abs).then_inc(av_ready, 1)
                act.wait_ge(av_ready, b + 1)
                nc.scalar.activation(ta2, ta2, ACT.Exp, scale=-1.0).then_inc(e_ready, 1)
                act.wait_ge(e_ready, b + 1)
                nc.scalar.activation(td[:, :, :], ta2, ACT.Ln, bias=1.0).then_inc(lw_ready, 1)
                act.wait_ge(delta_ready, b + 1)
                for n in range(NSTATE):
                    act.wait_ge(fill, fill_no(b, f"C{n}") + 1)
                    act.wait_ge(prod_ready, PRIMED + b * NSTATE + max(n - C_SLOTS + 1, 0))
                    nc.scalar.copy(Csb[:, n % C_SLOTS, :], PF).then_inc(drained, 1)
                    for a in range(HALVES):
                        i = n * HALVES + a
                        act.wait_ge(scanned, PRIMED + b * NSTATE * HALVES + max(i - DA_SLOTS + 1, 0))
                        nc.scalar.activation(dA[:, i % DA_SLOTS, :], delta[:, a, :], ACT.Exp,
                                             scale=A[:, a, n:n + 1]).then_inc(da_ready, 1)
                act.wait_ge(summed, PRIMED + NSTATE * (b + 1))
                nc.scalar.copy(ta2.rearrange("p a s -> p (a s)"), PY).then_inc(y_out, 1)
                act.wait_ge(o_filled, b + 1)
                nc.scalar.activation(tc[:, 0, :], PB, ACT.Identity, scale=mod[:, 2, ds(b, 1)],
                                     bias=gabo[:, ds(b, 1)]).then_inc(o_ready, 1)
                norm(b, 1)
            act.wait_ge(top_step, 2)
            nc.scalar.activation(lg, lg, ACT.Exp).then_inc(lexp, 1)
            with act.Fori(0, NTILE) as j:
                for e in range(EXPERTS):
                    for c, (i0, k) in enumerate(INNER):
                        s = e * NIN + c
                        act.wait_ge(g_filled, j * STEPS + s + 1)
                        act.wait_ge(inner_ready, PRIMED + j * STEPS + max(s - 1, 0))
                        nc.scalar.activation(silu[0:k, s % 2, :], PG(s)[0:k, :], ACT.Silu).then_inc(silu_ready, 1)
                act.wait_ge(down_done, PRIMED + STEPS * (j + 1))
                nc.scalar.activation(moe[:, :], PO, ACT.Copy, scale=gb8[:, ds(j, 1)]).then_inc(moe_scaled, 1)

        @block.vector
        def _(dve):
            def norm(b, k):
                i = b * NORMS + k + 1
                dve.wait_ge(fill, fill_no(b, f"mean{k}") + 1)
                dve.wait_ge(h2_ready, PRIMED + b)
                nc.vector.tensor_tensor(xc[:, :], xT[:, ds(b * SEQ, SEQ)], PF, ALU.subtract).then_inc(drained, 1)
                dve.wait_ge(drained, PRIMED + fill_no(b, f"mean{k}") + 1)
                dve.wait_ge(var_ready, i)
                nc.vector.tensor_scalar(small[:, 0, :], PS[:, 0:CH], LN_EPS, None, ALU.add).then_inc(v_ready, 1)
                dve.wait_ge(y0_ready, i)
                n0 = (i - 1) * 3
                nc.vector.tensor_tensor(small[:, 3, :], small[:, 0, :], small[:, 2, :], ALU.mult).then_inc(newton, 1)
                dve.wait_ge(newton, n0 + 1)
                nc.vector.tensor_tensor(small[:, 4, :], small[:, 3, :], small[:, 2, :], ALU.mult).then_inc(newton, 1)
                dve.wait_ge(newton, n0 + 2)
                nc.vector.tensor_scalar(small[:, 3, :], small[:, 4, :], -0.5, 1.5, ALU.mult, ALU.add).then_inc(newton, 1)
                dve.wait_ge(newton, n0 + 3)
                nc.vector.tensor_tensor(small[:, 5, :], small[:, 3, :], small[:, 2, :], ALU.mult).then_inc(rstd_ready, 1)
                dve.wait_ge(fill, fill_no(b, f"rstd{k}") + 1)
                nc.vector.tensor_tensor(xc[:, :], xc[:, :], PF, ALU.mult).then_inc(drained, 1)

            nc.vector.memset(mean_w[:, :], 1.0 / HID).then_inc(const_ready, 1)
            dve.wait_ge(mod_filled, 1)
            nc.vector.tensor_copy(mod[:, :, :], PB[:, 0:6 * BATCH].rearrange("p (k b) -> p k b", k=6)).then_inc(mod_step, 1)
            dve.wait_ge(mod_step, 1)
            gates = mod[:, 2:6:3, :]
            nc.vector.tensor_scalar(modt[:, :, :], gates, -1.0, 0.25, ALU.mult, ALU.max).then_inc(mod_step, 1)
            dve.wait_ge(mod_step, 2)
            nc.vector.tensor_tensor(modt[:, :, :], modt[:, :, :], gates, ALU.max).then_inc(mod_step, 1)
            nc.vector.tensor_scalar(mod[:, 1:5:3, :], mod[:, 1:5:3, :], 1.0, None, ALU.add).then_inc(mod_step, 1)
            dve.wait_ge(mod_step, 4)
            nc.vector.tensor_scalar(gates, gates, 0.0, 2.0, ALU.is_ge, ALU.mult).then_inc(mod_step, 1)
            dve.wait_ge(mod_step, 5)
            nc.vector.scalar_tensor_tensor(gates, gates, -1.0, modt[:, :, :], ALU.add, ALU.mult).then_inc(mod_step, 1)
            dve.wait_ge(mod_step, 6)
            nc.vector.tensor_scalar(gabo[:, :], mod[:, 2, :], bo[:, 0:1], None, ALU.mult).then_inc(mod_step, 1)
            nc.vector.tensor_copy(gb8[:, :].rearrange("p (b r) -> p b r", b=BATCH),
                                  mod[:, 5, :].unsqueeze(2).to_broadcast([P, BATCH, NTILE // BATCH])).then_inc(mod_step, 1)
            dve.wait_ge(load["attn"], 16 * 9)
            dve.wait_ge(ident_ready, 1)
            for a in range(HALVES):
                nc.vector.tensor_scalar(Ddiag[:, a, :], ident[:, :], cols[:, 4, a:a + 1], None, ALU.mult).then_inc(mod_step, 1)
            dve.wait_ge(a_exp, 1)
            nc.vector.tensor_scalar(A[:, :, :], A[:, :, :], -1.0, None, ALU.mult).then_inc(mod_step, 1)
            dve.wait_ge(mod_step, MOD_STEPS)
            dve.wait_ge(load["x"], 16)

            def shared_read(b, name):
                dve.wait_ge(fill, fill_no(b, name) + 1)

            with dve.Fori(0, BATCH) as b:
                norm(b, 0)
                nc.vector.memset(ubpad, 0.0).then_inc(ub_ready, 1)
                dve.wait_ge(ub_ready, b + 1)
                dve.wait_ge(drained, PRIMED + fill_no(b, "u1") + 1)
                for a in range(HALVES):
                    nc.vector.tensor_scalar(tb[:, a, :], ub[:, a, 0:SEQ], conv[:, a, 0:1], cols[:, 2, a:a + 1],
                                            ALU.mult, ALU.add).then_inc(conv_step, 1)
                for k in range(1, CONVK):
                    for a in range(HALVES):
                        dve.wait_ge(conv_step, b * CONVK * HALVES + (k - 1) * HALVES + a + 1)
                        last = nc.vector.scalar_tensor_tensor(tb[:, a, :], ub[:, a, k:k + SEQ], conv[:, a, k:k + 1],
                                                              tb[:, a, :], ALU.mult, ALU.add)
                        last.then_inc(conv_step, 1)
                dve.wait_ge(bc_filled, b + 1)
                nc.vector.tensor_copy(bcT[:, :, :], PS[:, 0:CH * 2 * NSTATE].rearrange("p (c m) -> p c m", c=CH)
                                      ).then_inc(bc_ready, 1)
                dve.wait_ge(e_ready, b + 1)
                t0 = b * 4
                nc.vector.tensor_scalar(tb[:, :, :], ta2, 1.0, 1.0, ALU.add, ALU.subtract).then_inc(sp_step, 1)
                dve.wait_ge(sp_step, t0 + 1)
                nc.vector.tensor_tensor(delta[:, :, :], ta2, tb[:, :, :], ALU.subtract).then_inc(sp_step, 1)
                dve.wait_ge(sp_step, t0 + 2)
                nc.vector.scalar_tensor_tensor(delta[:, :, :], tc[:, :, :], 0.0, delta[:, :, :], ALU.max, ALU.add
                                               ).then_inc(sp_step, 1)
                dve.wait_ge(lw_ready, b + 1)
                nc.vector.scalar_tensor_tensor(tb[:, :, :], tb[:, :, :], 0.0, td[:, :, :], ALU.is_gt, ALU.mult
                                               ).then_inc(sp_step, 1)
                dve.wait_ge(sp_step, t0 + 4)
                nc.vector.tensor_tensor(delta[:, :, :], delta[:, :, :], tb[:, :, :], ALU.add).then_inc(delta_ready, 1)
                dve.wait_ge(delta_ready, b + 1)
                nc.vector.tensor_tensor(du[:, :, :], delta[:, :, :], u[:, :, :], ALU.mult).then_inc(du_ready, 1)
                dve.wait_ge(du_ready, b + 1)
                for n in range(NSTATE):
                    step = b * NSTATE + n
                    s = scan_slot(n)
                    dve.wait_ge(b_filled, step + 1)
                    dve.wait_ge(summed, PRIMED + b * NSTATE + max(n - SCAN_SLOTS + 1, 0))
                    nc.vector.tensor_tensor(ring[:, s], du[:, :, :], PB.unsqueeze(1).to_broadcast([P, HALVES, SEQ]),
                                            ALU.mult).then_inc(dbu_ready, 1)
                    dve.wait_ge(dbu_ready, PRIMED + step + 1)
                    for a in range(HALVES):
                        i = n * HALVES + a
                        dve.wait_ge(da_ready, b * NSTATE * HALVES + i + 1)
                        nc.vector.tensor_tensor_scan(ring[:, s, a, :], dA[:, i % DA_SLOTS, :], ring[:, s, a, :], 0.0,
                                                     ALU.mult, ALU.add).then_inc(scanned, 1)
                for a in range(HALVES):
                    shared_read(b, f"yT{a}")
                    nc.vector.tensor_tensor(tb[:, a, :], gate[:, a, :], PF, ALU.mult).then_inc(drained, 1)
                dve.wait_ge(o_ready, b + 1)
                nc.vector.tensor_tensor(xT[:, ds(b * SEQ, SEQ)], xT[:, ds(b * SEQ, SEQ)], tc[:, 0, :], ALU.add
                                        ).then_inc(x1_ready, 1)
                norm(b, 1)
                dve.wait_ge(logit_filled, b + 1)
                nc.vector.tensor_copy(logits[:, ds(b, 1), :, :].rearrange("p b c e -> p (b c) e"),
                                      PS[:, 0:CH * EXPERTS].rearrange("p (c e) -> p c e", c=CH)).then_inc(logit_ready, 1)
            NG = BATCH * CH
            def per_token(v):
                return v.unsqueeze(2).to_broadcast([P, NG, EXPERTS])
            dve.wait_ge(logit_ready, PRIMED + BATCH)
            nc.vector.reduce_max(stat[:, 0, :], lg, mybir.AxisListType.X).then_inc(top_step, 1)
            dve.wait_ge(top_step, 1)
            nc.vector.tensor_tensor(lg, lg, per_token(stat[:, 0, :]), ALU.subtract).then_inc(top_step, 1)
            dve.wait_ge(lexp, 1)
            nc.vector.reduce_sum(stat[:, 0, :], lg, mybir.AxisListType.X).then_inc(top_step, 1)
            dve.wait_ge(top_step, 3)
            nc.vector.reciprocal(stat[:, 1, :], stat[:, 0, :]).then_inc(top_step, 1)
            dve.wait_ge(top_step, 4)
            nc.vector.tensor_tensor(lg, lg, per_token(stat[:, 1, :]), ALU.mult).then_inc(top_step, 1)
            dve.wait_ge(top_step, 5)
            pairs = [P, NG, EXPERTS, EXPERTS]
            other, own = lg.unsqueeze(2).to_broadcast(pairs), lg.unsqueeze(3).to_broadcast(pairs)
            ahead, ties = [t[:, :, :].rearrange("p a s -> p (a s)").rearrange("p (g e f) -> p g e f", g=NG, e=EXPERTS)
                           for t in (tb, tc)]
            nc.vector.tensor_tensor(ahead, other, own, ALU.is_gt).then_inc(top_step, 1)
            nc.vector.tensor_tensor(ties, other, own, ALU.is_equal).then_inc(top_step, 1)
            dve.wait_ge(top_step, 7)
            nc.vector.tensor_tensor(ties, ties, before[:, :, :].unsqueeze(1).to_broadcast(pairs), ALU.mult).then_inc(top_step, 1)
            dve.wait_ge(top_step, 8)
            nc.vector.tensor_tensor(ahead, ahead, ties, ALU.add).then_inc(top_step, 1)
            dve.wait_ge(top_step, 9)
            nc.vector.reduce_sum(wte[:, :, :], ahead, mybir.AxisListType.X).then_inc(top_step, 1)
            dve.wait_ge(top_step, 10)
            nc.vector.scalar_tensor_tensor(wte[:, :, :], wte[:, :, :], 2.0, lg, ALU.is_lt, ALU.mult).then_inc(top_step, 1)
            dve.wait_ge(top_step, 11)
            with dve.Fori(0, NTILE) as j:
                dve.wait_ge(wb_filled, PRIMED + j * EXPERTS)
                nc.vector.tensor_copy(wt[:, :, :], wte[:, ds(j * TCH, TCH), :]).then_inc(wt_ready, 1)
                for e in range(EXPERTS):
                    def weigh(e):
                        dve.wait_ge(wb_filled, PRIMED + j * EXPERTS + e + 1)
                        nc.vector.tensor_tensor(xw[:, e % 2, :], h2T[:, ds(j * TILE, TILE)], PW(e), ALU.mult
                                                ).then_inc(xw_ready, 1)
                    if e == 0:
                        weigh(0)
                    for c, (i0, k) in enumerate(INNER):
                        s = e * NIN + c
                        dve.wait_ge(silu_ready, PRIMED + j * STEPS + s + 1)
                        dve.wait_ge(up_filled, j * STEPS + s + 1)
                        dve.wait_ge(down_done, PRIMED + j * STEPS + max(s - 1, 0))
                        nc.vector.tensor_tensor(inner[0:k, s % 2, :], silu[0:k, s % 2, :], PU(s)[0:k, :], ALU.mult
                                                ).then_inc(inner_ready, 1)
                        if c == 0 and e + 1 < EXPERTS:
                            weigh(e + 1)
                dve.wait_ge(moe_scaled, PRIMED + j + 1)
                nc.vector.tensor_tensor(xT[:, ds(j * TILE, TILE)], xT[:, ds(j * TILE, TILE)], moe[:, :], ALU.add
                                        ).then_inc(out_ready, 1)


def kernel(**inputs):
    import numpy as np
    import concourse.bacc as bacc
    from concourse import mybir as mb
    from concourse.bass_utils import run_bass_kernel_spmd

    a = {k: np.asarray(v) for k, v in inputs.items()}
    at, ff = "L0_attn_", "L0_ffn_"
    columns = np.stack([a[at + k].reshape(HALVES, P) for k in ("b1", "b2", "conv_b", "dt_proj_b", "D_skip")])
    arrays = {
        "xT": a[at + "x"].reshape(NTOK, HID).T,
        "w1": a[at + "W1"], "w2": a[at + "W2"], "wo": a[at + "Wo"],
        "xproj": a[at + "x_proj_w"], "dtw": a[at + "dt_proj_w"], "alog": a[at + "A_log"], "conv": a[at + "conv_w"],
        "cols": columns.transpose(2, 0, 1).reshape(P, 5 * HALVES), "bo": a[at + "bo"].reshape(P, 1),
        "router": a[ff + "router_w"].T,
        "gate": a[ff + "gate_w"].reshape(EXPERTS * INTER, HID).T,
        "up": a[ff + "up_w"].reshape(EXPERTS * INTER, HID).T,
        "down": a[ff + "down_w"].transpose(0, 2, 1).reshape(EXPERTS * INTER, HID),
        "cT": a["L0_c"].T, "wmod": a["L0_wmod"],
    }
    arrays = {f"in_{k}": np.ascontiguousarray(v) for k, v in arrays.items()}
    nc = bacc.Bacc("TRN2", target_bir_lowering=False, num_devices=1)
    args = [nc.dram_tensor(k, v.shape, mb.dt.from_np(v.dtype), kind="ExternalInput").ap() for k, v in arrays.items()]
    out = nc.dram_tensor("out_T", (HID, NTOK), mb.dt.float32, kind="ExternalOutput").ap()
    adaln_kernel(nc, *args, out)
    r = run_bass_kernel_spmd(nc, [arrays], core_ids=[0])
    return np.ascontiguousarray(np.asarray(r.results[0]["out_T"]).T).reshape(BATCH, SEQ, HID)
```

```python
from contextlib import ExitStack

import concourse.bass as bass
from concourse import mybir

fp32 = mybir.dt.float32
fp32r = mybir.dt.float32r
int32 = mybir.dt.int32
ALU = mybir.AluOpType
ACT = mybir.ActivationFunctionType
AX = mybir.AxisListType
ds = bass.ds

P = 128
BATCH, SEQ, HID = 4, 1024, 128
MLP, NSTATE, DTRANK, CONVK = 256, 16, 64, 4
EXPERTS, INTER, TOPK = 8, 352, 2
NTOK = BATCH * SEQ
HALVES = MLP // P
BANK = 512
CH = SEQ // P
SEG = SEQ // BANK
LN_EPS = 1e-5
PROJ = DTRANK + 2 * NSTATE
GAPS = 2 * NSTATE
RING, DA_SLOTS, C_SLOTS = 4, 4, 2

INNER = [(c * P, min(P, INTER - c * P)) for c in range(-(-INTER // P))]
NIN = len(INNER)
XS_SLOTS = 4
ROW_TILES = -(-(TOPK * SEQ // P + EXPERTS - 1) // XS_SLOTS) * XS_SLOTS
ROW_SLOTS = ROW_TILES * P
TILES = BATCH * ROW_TILES
TAIL_GAP = 4
DVE_PRODUCTS = (6, 10, 13, 15)
COMBINE_LAG = 20


def wait(eng, signal, count):
    if not (isinstance(count, int) and count <= 0):
        eng.wait_ge(signal, count)


def value(eng, count):
    return count if isinstance(count, int) else eng.snap(eng.to_reg(count))


def adaln_kernel(nc, xT_d, w1_d, w2_d, wo_d, xproj_d, dtw_d, alog_d, conv_d, cols_d, bo_d, router_d,
                 gate_d, up_d, down_d, cT_d, wmod_d, outT_d, xs_d, ys_d):
    ctx = ExitStack()
    with ctx:
        def sb(name, shape, dt=fp32):
            return ctx.enter_context(nc.sbuf_tensor(name, shape, dt))

        def sem(name):
            return ctx.enter_context(nc.semaphore(name))

        xT = sb("xT", [P, NTOK])
        ident = sb("ident", [P, P])
        mean_w = sb("mean_w", [P, P])
        ones = sb("ones", [P, P])
        below = sb("below", [P, P])
        pick = sb("pick", [2 * 2 * NSTATE, 2 * NSTATE], fp32r)
        w1 = sb("w1", [P, MLP])
        w2 = sb("w2", [P, MLP])
        wo = sb("wo", [P, HALVES, HID])
        xproj = sb("xproj", [P, HALVES, PROJ])
        dtw = sb("dtw", [DTRANK, MLP])
        A = sb("A", [P, HALVES, NSTATE])
        conv = sb("conv", [P, HALVES, CONVK])
        cols = sb("cols", [P, 5, HALVES])
        b2half = sb("b2half", [P, HALVES])
        half = sb("half", [P, 1])
        bo = sb("bo", [P, 1])
        Ddiag = sb("Ddiag", [P, HALVES, P])
        router = sb("router", [P, EXPERTS])
        cT = sb("cT", [P, BATCH])
        siluc = sb("siluc", [P, BATCH])
        mod = sb("mod", [P, 6, BATCH])
        modt = sb("modt", [P, 2, BATCH])
        gabo = sb("gabo", [P, BATCH])
        gahalf = sb("gahalf", [P, BATCH])
        before = sb("before", [P, EXPERTS, EXPERTS])
        tile_i = sb("tile_i", [P, ROW_TILES], int32)
        tile_f = sb("tile_f", [P, ROW_TILES])
        rowbase = sb("rowbase", [P, 1])
        xcsq = sb("xcsq", [P, 2, SEQ])
        xc, sq = xcsq[:, 0, :], xcsq[:, 1, :]
        hT = sb("hT", [P, SEQ])
        h2r = sb("h2r", [P, CH, HID])
        PADW = SEQ + P
        ubm = sb("ubm", [P, HALVES * PADW])
        z = sb("z", [P, HALVES, SEQ])
        ROWW = HALVES * SEQ
        stream = sb("stream", [P, ROWW + 2 * 2 * ROWW])
        u = stream[:, 0:ROWW].rearrange("p (a s) -> p a s", a=HALVES)
        dd = stream[:, ROWW:].rearrange("p (r k a s) -> p r k a s", r=2, k=2, a=HALVES)
        gate = sb("gate", [P, 2, HALVES, SEQ])
        xdt = sb("xdt", [DTRANK, SEQ])
        bcs = sb("bcs", [2 * 2 * NSTATE, 2, SEQ], fp32r)
        ysb = sb("ysb", [P, CH, MLP])
        Csb = sb("Csb", [P, C_SLOTS, SEQ])
        dA = sb("dA", [P, DA_SLOTS, SEQ])
        ring = sb("ring", [P, RING, HALVES, SEQ])
        small = sb("small", [P, 6, CH])
        RW = CH * EXPERTS
        prob = sb("prob", [P, RW])
        stat = sb("stat", [P, 2, CH])
        ahead = sb("ahead", [P, RW * EXPERTS])
        ties = sb("ties", [P, RW * EXPERTS])
        rank = sb("rank", [P, RW])
        chosen = sb("chosen", [P, TOPK, RW])
        both = sb("both", [P, RW])
        picked = sb("picked", [P, TOPK, RW])
        HEAD = CH // 2
        sums = sb("sums", [P, 2, HEAD + CH, EXPERTS])
        ntile_i = sb("ntile_i", [P, EXPERTS], int32)
        ntile = sb("ntile", [P, EXPERTS])
        starts = sb("starts", [P, EXPERTS])
        ends = sb("ends", [P, EXPERTS])
        pairs8 = sb("pairs8", [P, EXPERTS, EXPERTS])
        slot_f = sb("slot_f", [P, RW])
        pos_f = sb("pos_f", [P, TOPK * CH])
        pos = sb("pos", [P, TOPK * CH], int32)
        pos_all = sb("pos_all", [P, BATCH, TOPK * CH], int32)
        pos_g = sb("pos_g", [P, TOPK * CH], int32)
        wsel = sb("wsel", [P, BATCH, TOPK * CH])
        past = sb("past", [P, ROW_TILES * EXPERTS])
        expert_f = sb("expert_f", [P, ROW_TILES])
        expert = sb("expert", [P, TILES], int32)

        ubv = ubm[:, :].rearrange("p (a s) -> p a s", a=HALVES)
        ub, ubpad = ubv[:, :, P - CONVK + 1:], ubv[:, :, P - CONVK + 1:P]
        yg = z
        o_sb = sq
        v_sb = z
        e_sb = ubm[:, 0:HALVES * SEQ].rearrange("p (a s) -> p a s", a=HALVES)
        w_sb = ysb[:, :, :].rearrange("p c m -> p (c m)").rearrange("p (a s) -> p a s", a=HALVES)
        lw_sb = xcsq
        wmod = ring[:, 0, 0, 0:6 * P].rearrange("p (k m) -> p k m", k=6)
        gate_w = stream[:, 0:EXPERTS * INTER]
        up_w = stream[:, EXPERTS * INTER:2 * EXPERTS * INTER]
        down_w = dA[:, :, :].rearrange("p r s -> p (r s)")[:, 0:NIN * EXPERTS * HID].rearrange("p (c m) -> p c m", c=NIN)
        gath = gate[:, :, :, :].rearrange("p r a s -> p r (a s)").rearrange("p r (j h) -> p r j h", h=HID)

        def tiles_of(area, at, count, width=P):
            return area[:, at:at + count * width].rearrange("p (k h) -> p k h", k=count)

        odd = stream[:, 3 * ROWW:]
        xs, xsT, ob = tiles_of(odd, 0, XS_SLOTS), tiles_of(odd, 4 * P, 2), tiles_of(odd, 6 * P, XS_SLOTS)
        innerT = tiles_of(odd, 10 * P, 2, NIN * P)
        th, sg, inner = (tiles_of(ubm, 2 * k * INTER, 2, INTER) for k in range(3))
        mix = xc.rearrange("p (c h) -> p c h", h=HID)

        psum = ctx.enter_context(nc.psum_tensor("psum", [P, 8 * BANK], fp32))

        def bank(i, n=1):
            return psum[:, i * BANK:(i + n) * BANK]

        PY = bank(0, 4)
        PYc = PY.rearrange("p (c m) -> p c m", c=CH)
        PBC = [bank(4), bank(5)]
        PF = bank(6, 2)
        PX, PU, PI, PO, PM = bank(0)[:, 0:P], bank(3), bank(4), bank(5)[:, 0:P], bank(7)

        def PG(k):
            return bank(1 + k % 2)

        PIECES = ["mean0", "var0", "rstd0", "yT0", "yT1", "wo", "u0", "u1", "mean1", "gate0", "gate1", "var1",
                  "rstd1", "logit", "rows", "xproj", "dt0", "dt1", "prefix"]
        filled = {n: sem(f"{n}_filled") for n in PIECES}
        read = {n: sem(f"{n}_read") for n in PIECES}
        READS = {"xproj": 3, "prefix": 2}

        loaded = {n: sem(f"load_{n}") for n in ("c", "attn", "gateup", "down")}
        loaded_x = [sem(f"loaded_x{b}") for b in range(BATCH)]
        zeroed = sem("zeroed")
        setup = sem("setup")
        siluc_ready, mod_filled, mod_step, a_exp = (sem(n) for n in ("siluc_ready", "mod_filled", "mod_step", "a_exp"))
        sq_ready = [sem(f"sq{k}_ready") for k in range(2)]
        lnv_ready = [sem(f"lnv{k}_ready") for k in range(2)]
        y0_ready = [sem(f"y0{k}_ready") for k in range(2)]
        newton = [sem(f"newton{k}") for k in range(2)]
        rstd_ready = [sem(f"rstd{k}_ready") for k in range(2)]
        h_ready = [sem(f"h{k}_ready") for k in range(2)]
        pad_clear, conv_step = sem("pad_clear"), [sem(f"conv_step{a}") for a in range(HALVES)]
        tanhz_ready, u_ready = sem("tanhz_ready"), sem("u_ready")
        av_ready, e_ready, lw_ready, w_ready, lost_ready, softplus_step, delta_ready, du_ready = (
            sem(n) for n in ("av_ready", "e_ready", "lw_ready", "w_ready", "lost_ready", "softplus_step", "delta_ready",
                             "du_ready"))
        b_filled, dbu_ready, c_filled, c_copied, da_ready, scanned, prod_ready, dve_prod_ready, summed = (
            sem(n) for n in ("b_filled", "dbu_ready", "c_filled", "c_copied", "da_ready", "scanned", "prod_ready", "dve_prod_ready",
                             "summed"))
        y_out, x1_ready = sem("y_out"), sem("x1_ready")
        route, prob_exp, chosen_ready, pos_ready, table_written, table_cleared, rowstep, wsum, wsel_ready, place, table = (
            sem(n) for n in ("route", "prob_exp", "chosen_ready", "pos_ready", "table_written", "table_cleared", "rowstep",
                             "wsum", "wsel_ready", "place", "table"))
        xs_loaded = [sem(f"xs_loaded{k}") for k in range(XS_SLOTS)]
        xt_filled, xt_read, g_filled, u_filled, tanh_ready, sg_ready, inner_ready, it_filled, it_read, o_filled, o_read = (
            sem(n) for n in ("xt_filled", "xt_read", "g_filled", "u_filled", "tanh_ready", "sg_ready", "inner_ready",
                             "it_filled", "it_read", "o_filled", "o_read"))
        ys_stored = [sem(f"ys_stored{k}") for k in range(XS_SLOTS)]
        gathered = [sem(f"gathered{c}") for c in range(CH)]
        pos_back, mixed, mt_filled, mt_read, stored = (
            sem(n) for n in ("pos_back", "mixed", "mt_filled", "mt_read", "stored"))

        ATTN_LOADS = 9
        SETUP = 8
        MOD_STEPS = 18
        block = ctx.enter_context(nc.Block())

        def writes(b):
            return 16 * b * TOPK * CH

        def scattered_before(eng, b):
            if isinstance(b, int):
                wait(eng, table_written, writes(b))
            else:
                eng.wait_ge(prod_ready, (b + 1) * NSTATE + 1)

        def on_dve(b, n):
            return isinstance(b, int) and b == BATCH - 1 and n in DVE_PRODUCTS

        def wait_product(eng, b, n):
            if n < 0:
                b, n = b - 1, n + NSTATE
            if isinstance(b, int) and b < 0:
                return
            if on_dve(b, n):
                eng.wait_ge(dve_prod_ready, DVE_PRODUCTS.index(n) + 1)
            else:
                own = sum(on_dve(b, m) for m in range(n))
                eng.wait_ge(prod_ready, b * NSTATE + n + 1 - own)

        def each_gap(b, work):
            for gap in range(GAPS):
                work(gap, b)

        def rows(first, inside, last, eng):
            first(0)
            with eng.Fori(1, BATCH - 1) as b:
                inside(b)
            last(BATCH - 1)

        def tile_schedule(eng, tile, beside, opened, combine):
            rounds = TILES // XS_SLOTS
            at = -(-(GAPS - TAIL_GAP) // 2 // XS_SLOTS)
            for t in range(at * XS_SLOTS):
                for gap in (TAIL_GAP + 2 * t, TAIL_GAP + 2 * t + 1):
                    if gap < GAPS:
                        beside(gap, BATCH - 1)
                tile(t, t % XS_SLOTS, t // XS_SLOTS)
            opened()
            for b in range(BATCH - 1):
                until = -(-((b + 1) * ROW_TILES + COMBINE_LAG) // XS_SLOTS)
                with eng.Fori(at, until) as i:
                    for k in range(XS_SLOTS):
                        tile(i * XS_SLOTS + k, k, i)
                combine(b)
                at = until
            if at < rounds - 1:
                with eng.Fori(at, rounds - 1) as i:
                    for k in range(XS_SLOTS):
                        tile(i * XS_SLOTS + k, k, i)
            for k in range(XS_SLOTS + 3):
                tile((rounds - 1) * XS_SLOTS + k, k, rounds - 1)
            combine(BATCH - 1)

        @block.sync
        def _(sp):
            sp.dma_start(cT[:, :], cT_d).then_inc(loaded["c"], 16)
            sp.dma_start(wmod, wmod_d.rearrange("h (k m) -> h k m", k=6)).then_inc(loaded["c"], 16)
            sp.dma_start(bo[:, :], bo_d).then_inc(loaded["c"], 16)
            sp.dma_start(xT[:, 0:SEQ], xT_d[:, 0:SEQ]).then_inc(loaded_x[0], 16)
            sp.dma_start(w1[:, :], w1_d).then_inc(loaded["attn"], 16)
            sp.dma_start(w2[:, :], w2_d).then_inc(loaded["attn"], 16)
            sp.dma_start(wo[:, :, :], wo_d.rearrange("(a p) m -> p a m", p=P)).then_inc(loaded["attn"], 16)
            sp.dma_start(xproj[:, :, :], xproj_d.rearrange("(a p) m -> p a m", p=P)).then_inc(loaded["attn"], 16)
            sp.dma_start(dtw[:, :], dtw_d).then_inc(loaded["attn"], 16)
            sp.dma_start(A[:, :, :], alog_d.rearrange("(a p) m -> p a m", p=P)).then_inc(loaded["attn"], 16)
            sp.dma_start(conv[:, :, :], conv_d.rearrange("(a p) m -> p a m", p=P)).then_inc(loaded["attn"], 16)
            sp.dma_start(cols[:, :, :], cols_d.rearrange("p (k a) -> p k a", k=5)).then_inc(loaded["attn"], 16)
            sp.dma_start(router[:, :], router_d).then_inc(loaded["attn"], 16)
            for b in range(1, BATCH):
                sp.dma_start(xT[:, b * SEQ:(b + 1) * SEQ], xT_d[:, b * SEQ:(b + 1) * SEQ]).then_inc(loaded_x[b], 16)
            sp.wait_ge(zeroed, 1)
            for b in range(BATCH):
                table_, at = xs_d[b // (BATCH - 1)], b % (BATCH - 1) * ROW_SLOTS
                sp.dma_start(table_[at:at + ROW_SLOTS, :].rearrange("(k p) h -> p k h", p=P),
                             h2r[:, 0:1, :].to_broadcast([P, ROW_TILES, HID])).then_inc(table_cleared, 16)
            sp.wait_ge(summed, (BATCH - 1) * NSTATE + 1)
            sp.dma_start(gate_w, gate_d).then_inc(loaded["gateup"], 16)
            sp.dma_start(up_w, up_d).then_inc(loaded["gateup"], 16)
            sp.wait_ge(scanned, BATCH * NSTATE * HALVES)
            sp.wait_ge(table_written, writes(BATCH - 1))
            rounds, row_rounds = TILES // XS_SLOTS, ROW_TILES // XS_SLOTS

            def load(i, k, last_row):
                if not isinstance(i, int) or i > 0:
                    sp.wait_ge(xt_filled, i * XS_SLOTS + (k + 1 - XS_SLOTS))
                first = (BATCH - 1) * ROW_TILES if last_row else 0
                sp.dma_start(xs[:, k, :], xs_d[int(last_row)][ds((i * XS_SLOTS + k - first) * P, P), :]
                             ).then_inc(xs_loaded[k], 16)

            for k in range(XS_SLOTS):
                load(0, k, False)
            for c, (i0, k) in enumerate(INNER):
                sp.dma_start(down_w[0:k, c, :].rearrange("i (e h) -> i e h", e=EXPERTS),
                             down_d.rearrange("(e i) h -> i e h", e=EXPERTS)[i0:i0 + k, :, :]).then_inc(loaded["down"], 16)

            def store(i, k, b):
                sp.wait_ge(o_read, i * XS_SLOTS + (k + 1))
                sp.dma_start(ys_d[b][ds((i * XS_SLOTS + k - b * ROW_TILES) * P, P), :], ob[:, k, :]
                             ).then_inc(ys_stored[k], 16)

            for k in range(XS_SLOTS):
                load(1, k, False)
            last_load = (BATCH - 1) * row_rounds - 2
            cuts = sorted({b * row_rounds for b in range(BATCH)} | {last_load, rounds - 2})
            for first, end in zip(cuts, cuts[1:]):
                if first == last_load:
                    sp.wait_ge(table_written, writes(BATCH))
                with sp.Fori(first, end) as i:
                    for k in range(XS_SLOTS):
                        load(i + 2, k, first >= last_load)
                        store(i, k, first // row_rounds)
            for i in (rounds - 2, rounds - 1):
                for k in range(XS_SLOTS):
                    store(i, k, BATCH - 1)
            for k in range(XS_SLOTS):
                sp.wait_ge(ys_stored[k], 16 * (TILES // XS_SLOTS))

        @block.gpsimd
        def _(pool):
            nc.gpsimd.memset(h2r[:, :, :], 0.0).then_inc(zeroed, 1)
            nc.gpsimd.memset(ident[:, :], 0.0).then_inc(setup, 1)
            nc.gpsimd.memset(below[:, :], 1.0).then_inc(setup, 1)
            nc.gpsimd.memset(before[:, :, :], 1.0).then_inc(setup, 1)
            nc.gpsimd.memset(ones[:, :], 1.0).then_inc(setup, 1)
            nc.gpsimd.iota(tile_i[:, :], pattern=[[1, ROW_TILES]], base=0, channel_multiplier=0).then_inc(setup, 1)
            pool.wait_ge(setup, 5)
            nc.gpsimd.affine_select(out=ident[:, :], in_=ident[:, :], compare_op=ALU.not_equal, fill=1.0, base=0,
                                    pattern=[[-1, P]], channel_multiplier=1).then_inc(setup, 1)
            nc.gpsimd.affine_select(out=below[:, :], in_=below[:, :], compare_op=ALU.is_gt, fill=0.0, base=0,
                                    pattern=[[1, P]], channel_multiplier=-1).then_inc(setup, 1)
            nc.gpsimd.affine_select(out=before[:, :, :], in_=before[:, :, :], compare_op=ALU.is_gt, fill=0.0, base=0,
                                    pattern=[[1, EXPERTS], [-1, EXPERTS]], channel_multiplier=0).then_inc(setup, 1)

            def tail(gap, b):
                if gap == 23:
                    row = value(pool, b + 1)
                    pool.wait_ge(table_cleared, 16 * BATCH)
                    pool.wait_ge(pos_ready, row)
                    pool.wait_ge(read["rows"], row)
                if 23 <= gap < 23 + CH:
                    c = gap - 23
                    for j in range(TOPK):
                        i = j * CH + c
                        table_ = xs_d[int(isinstance(b, int) and b == BATCH - 1)]
                        nc.gpsimd.indirect_dma_start(table_, bass.IndirectOffsetOnAxis(ap=pos[:, i:i + 1], axis=0),
                                                     h2r[:, c, :], None).then_inc(table_written, 16)
                if gap == GAPS - 1:
                    pool.wait_ge(table_written, writes(b + 1))

            def scan(b, tail_b):
                for n in range(NSTATE):
                    step = b * NSTATE + n
                    if not on_dve(b, n):
                        pool.wait_ge(scanned, (step + 1) * HALVES)
                        pool.wait_ge(c_copied, (step + 1) * SEG)
                        nc.gpsimd.tensor_tensor(ring[:, n % RING], ring[:, n % RING],
                                                Csb[:, n % C_SLOTS, :].unsqueeze(1).to_broadcast([P, HALVES, SEQ]),
                                                ALU.mult).then_inc(prod_ready, 1)
                    for gap in (2 * n, 2 * n + 1):
                        if tail_b is not None:
                            tail(gap, tail_b)

            rows(lambda b: scan(b, None), lambda b: scan(b, b - 1), lambda b: scan(b, b - 1), pool)
            each_gap(BATCH - 1, tail)
            for b in range(BATCH):
                pool.wait_ge(table_written, writes(BATCH))
                for k in range(XS_SLOTS):
                    pool.wait_ge(ys_stored[k], 16 * (ROW_TILES // XS_SLOTS) * (b + 1))
                pool.wait_ge(pos_back, b + 1)
                wait(pool, mixed, b * TOPK * CH)
                for i in [j * CH + c for c in range(CH) for j in range(TOPK)]:
                    nc.gpsimd.indirect_dma_start(gath[:, 0, i, :], None, ys_d[b],
                                                 bass.IndirectOffsetOnAxis(ap=pos_g[:, i:i + 1], axis=0)
                                                 ).then_inc(gathered[i % CH], 16)

        @block.tensor
        def _(pe):
            def product(out, lhsT, rhs, start=True, stop=True):
                return nc.tensor.matmul(out, lhsT, rhs, start=start, stop=stop)

            def turn(out, block_in, start=True):
                return nc.tensor.matmul(out, block_in, ident[0:block_in.shape[0], 0:block_in.shape[0]],
                                        is_transpose=True, start=start, stop=True, skip_group_check=True)

            before_fill = [None]

            def fill(name, b, work):
                if before_fill[0]:
                    pe.wait_ge(*before_fill[0])
                work().then_inc(filled[name], 1)
                before_fill[0] = (read[name], READS.get(name, 1) * (b + 1))

            def mean(b, k):
                def work():
                    for g in range(SEG):
                        last = product(PF[:, g * BANK:(g + 1) * BANK], mean_w[:, :], xT[:, ds(b * SEQ + g * BANK, BANK)])
                    return last
                fill(f"mean{k}", b, work)

            def var(b, k):
                pe.wait_ge(sq_ready[k], b + 1)

                def work():
                    for c in range(CH):
                        last = product(PF[:, c:c + 1], sq[:, c * P:(c + 1) * P], mean_w[:, 0:1])
                    return last
                fill(f"var{k}", b, work)

            def rstd(b, k):
                pe.wait_ge(rstd_ready[k], b + 1)

                def work():
                    for c in range(CH):
                        last = turn(PF[:, c * P:(c + 1) * P], small[:, 5, c:c + 1].to_broadcast([P, P]))
                    return last
                fill(f"rstd{k}", b, work)

            def from_h(name, b, w, a):
                def work():
                    for g in range(SEG):
                        last = product(PF[:, g * BANK:(g + 1) * BANK], w[:, a * P:(a + 1) * P],
                                       hT[:, g * BANK:(g + 1) * BANK])
                    return last
                fill(f"{name}{a}", b, work)

            def front(gap, b):
                if gap == 0:
                    if isinstance(b, int):
                        pe.wait_ge(loaded_x[b], 16)
                    else:
                        for row in range(BATCH):
                            pe.wait_ge(loaded_x[row], 16)
                    mean(b, 0)
                if gap == 3:
                    var(b, 0)
                if gap == 6:
                    rstd(b, 0)
                if gap == 8:
                    pe.wait_ge(h_ready[0], b + 1)
                if gap in (8, 10):
                    from_h("u", b, w1, gap // 2 - 4)
                if gap in (12, 14):
                    from_h("gate", b, w2, gap // 2 - 6)
                if gap == 19:
                    pe.wait_ge(u_ready, b + 1)

                    def work():
                        for g in range(SEG):
                            for a in range(HALVES):
                                last = product(PF[0:PROJ, g * BANK:(g + 1) * BANK], xproj[:, a, :],
                                               u[:, a, g * BANK:(g + 1) * BANK], a == 0, a == HALVES - 1)
                        return last
                    fill("xproj", b, work)
                if gap in (21, 23):
                    a = gap // 2 - 10

                    def work():
                        for g in range(SEG):
                            last = product(PF[:, g * BANK:(g + 1) * BANK], dtw[:, a * P:(a + 1) * P],
                                           xdt[:, g * BANK:(g + 1) * BANK])
                        return last
                    fill(f"dt{a}", b, work)

            def tail(gap, b):
                if gap in (4, 5):
                    a = gap - 4
                    pe.wait_ge(y_out, b + 1)

                    def work():
                        for c in range(CH):
                            last = turn(PF[:, c * P:(c + 1) * P], ysb[:, c, a * P:(a + 1) * P])
                        return last
                    fill(f"yT{a}", b, work)
                if gap == 9:
                    pe.wait_ge(read["yT1"], b + 1)

                    def work():
                        for g in range(SEG):
                            for a in range(HALVES):
                                last = product(PF[:, g * BANK:(g + 1) * BANK], wo[:, a, :],
                                               yg[:, a, g * BANK:(g + 1) * BANK], a == 0, a == HALVES - 1)
                        return last
                    fill("wo", b, work)
                if gap == 11:
                    pe.wait_ge(x1_ready, b + 1)
                    mean(b, 1)
                if gap == 13:
                    var(b, 1)
                if gap == 15:
                    rstd(b, 1)
                if gap == 17:
                    pe.wait_ge(h_ready[1], b + 1)

                    def work():
                        for c in range(CH):
                            last = product(PF[:, c * EXPERTS:(c + 1) * EXPERTS], hT[:, c * P:(c + 1) * P], router[:, :])
                        return last
                    fill("logit", b, work)
                if gap == 18:
                    def work():
                        for c in range(CH):
                            last = turn(PF[:, c * P:(c + 1) * P], hT[:, c * P:(c + 1) * P])
                        return last
                    fill("rows", b, work)
                if gap == 22:
                    pe.wait_ge(chosen_ready, b + 1)

                    def work():
                        product(PF[:, 0:RW], below[:, :], both[:, :])
                        return product(PF[:, BANK:BANK + RW], ones[:, :], both[:, :])
                    fill("prefix", b, work)

            def add_state(b, n):
                wait_product(pe, b, n)
                for c in range(CH):
                    for a in range(HALVES):
                        last = turn(PYc[:, c, a * P:(a + 1) * P], ring[:, n % RING, a, c * P:(c + 1) * P], start=False)
                last.then_inc(summed, 1)

            def start_y(b):
                wait(pe, y_out, b)
                for c in range(CH):
                    for a in range(HALVES):
                        nc.tensor.matmul(PYc[:, c, a * P:(a + 1) * P], u[:, a, c * P:(c + 1) * P], Ddiag[:, a, :],
                                         start=(c % 2 == 0 and a == 0), stop=True, skip_group_check=True)

            def fill_row(b, row, g, out, signal, done, count):
                last_read = value(pe, count)
                pe.wait_ge(mod_step, MOD_STEPS)
                wait(pe, done, last_read)
                product(out[g], pick[:, row:row + 1].to_broadcast([2 * 2 * NSTATE, P]),
                        bcs[:, ds(b % 2, 1), g * BANK:(g + 1) * BANK].squeeze(1)).then_inc(signal, 1)

            def fill_b(b, n):
                for g in range(SEG):
                    fill_row(b, n, g, PBC, b_filled, c_copied, (b * NSTATE + n - 1) * SEG + g + 1)

            def fill_c(b, n):
                for g in range(SEG):
                    fill_row(b, NSTATE + n, g, PBC, c_filled, dbu_ready, (b * NSTATE + n) * SEG + g + 1)

            def scan(b, tail_b, front_b):
                before_fill[0] = (read["dt1"], b + 1)
                for n in range(NSTATE):
                    fill_c(b, n)
                    gap_work(2 * n, tail_b, front_b)
                    if n + 1 < NSTATE:
                        fill_b(b, n + 1)
                    elif front_b is not None:
                        fill_b(front_b, 0)
                    if n == 2:
                        start_y(b)
                    elif n > 2:
                        for m in ((0, 1) if n == 3 else (n - 2,)):
                            add_state(b, m)
                    elif tail_b is not None:
                        add_state(b - 1, NSTATE - 2 + n)
                    gap_work(2 * n + 1, tail_b, front_b)

            def gap_work(gap, tail_b, front_b):
                if front_b is not None:
                    front(gap, front_b)
                if tail_b is not None:
                    tail(gap, tail_b)

            pe.wait_ge(loaded["c"], 48)
            pe.wait_ge(siluc_ready, 1)
            for k in range(6):
                last = product(PBC[0][:, k * BATCH:(k + 1) * BATCH], wmod[:, k, :], siluc[:, :])
            last.then_inc(mod_filled, 1)
            pe.wait_ge(setup, SETUP)
            pe.wait_ge(loaded["attn"], 16 * ATTN_LOADS)
            pe.wait_ge(mod_step, MOD_STEPS)
            each_gap(0, front)
            fill_b(0, 0)
            rows(lambda b: scan(b, None, b + 1), lambda b: scan(b, b - 1, b + 1), lambda b: scan(b, b - 1, None), pe)
            for n in (NSTATE - 2, NSTATE - 1):
                add_state(BATCH - 1, n)
            before_fill[0] = (read["prefix"], READS["prefix"] * (BATCH - 1))

            pe.wait_ge(loaded["gateup"], 32)
            pe.wait_ge(table, 4 * (BATCH - 1))
            pe.wait_ge(y_out, BATCH)

            ahead_of = {}

            def expert_of(k, held):
                if held in ahead_of:
                    return ahead_of.pop(held)
                return pe.value_load(expert[0:1, ds(k, 1)], min_val=0, max_val=EXPERTS - 1)

            def gate_up(k, par, e):
                pe.wait_ge(xt_read, k + 1)
                wait(pe, sg_ready, k - 1)
                product(PG(par)[:, 0:INTER], xsT[:, par % 2, :], gate_w[:, ds(e * INTER, INTER)]).then_inc(g_filled, 1)
                wait(pe, inner_ready, k)
                product(PU[:, 0:INTER], xsT[:, par % 2, :], up_w[:, ds(e * INTER, INTER)]).then_inc(u_filled, 1)

            def turn_inner(k, par):
                pe.wait_ge(inner_ready, k + 1)
                wait(pe, it_read, k)
                for c, (i0, w) in enumerate(INNER):
                    last = turn(PI[0:w, c * P:(c + 1) * P], inner[:, par % 2, i0:i0 + w])
                last.then_inc(it_filled, 1)

            def down(k, par, e):
                if isinstance(k, int) and k == 0:
                    pe.wait_ge(loaded["down"], 16 * NIN)
                pe.wait_ge(it_read, k + 1)
                wait(pe, o_read, k)
                for c, (i0, w) in enumerate(INNER):
                    last = product(PO, innerT[0:w, par % 2, c * P:(c + 1) * P],
                                   down_w[0:w, c, ds(e * HID, HID)], c == 0, c == NIN - 1)
                last.then_inc(o_filled, 1)

            def combine(b):
                if b == BATCH - 3:
                    pe.wait_ge(table, 4 * BATCH)
                for g in range(SEG):
                    wait(pe, mt_read, b * SEG + g)
                    pe.wait_ge(mixed, (b * SEG + g + 1) * (CH // SEG * TOPK))
                    for c in range(CH // SEG):
                        last = turn(PM[:, c * P:(c + 1) * P], mix[:, g * (CH // SEG) + c, :])
                    last.then_inc(mt_filled, 1)

            def tile(k, par, rnd):
                static = isinstance(k, int)
                if not static or k < TILES:
                    e_gate = expert_of(k, "gate")
                if not static or 0 <= k - 3 < TILES:
                    e_down = expert_of(k - 3, "down")
                if not static or k + 1 < TILES:
                    slot = (par + 1) % XS_SLOTS
                    extra = 1 if par + 1 == XS_SLOTS else 0
                    pe.wait_ge(xs_loaded[slot], 16 * (rnd + extra + 1))
                    wait(pe, xt_read, k + 1)
                    turn(PX, xs[:, slot, :]).then_inc(xt_filled, 1)
                if not static or 0 <= k - 3 < TILES:
                    down(k - 3, par - 3, e_down)
                if not static or k < TILES:
                    gate_up(k, par, e_gate)
                if par % XS_SLOTS < XS_SLOTS - 1 or (static and k >= TILES - 1):
                    if not static or k + 1 < TILES:
                        ahead_of["gate"] = expert_of(k + 1, None)
                    if not static or 0 <= k - 2 < TILES:
                        ahead_of["down"] = expert_of(k - 2, None)
                if not static or 0 <= k - 1 < TILES:
                    turn_inner(k - 1, par - 1)

            pe.wait_ge(xs_loaded[0], 16)
            turn(PX, xs[:, 0, :]).then_inc(xt_filled, 1)
            tile_schedule(pe, tile, tail, lambda: None, combine)

        @block.scalar
        def _(act):
            def square(b, k):
                act.wait_ge(read[f"mean{k}"], b + 1)
                nc.scalar.activation(sq, xc, ACT.Square).then_inc(sq_ready[k], 1)

            def rsqrt_seed(b, k):
                act.wait_ge(read[f"var{k}"], b + 1)
                nc.scalar.activation(small[:, 1, :], small[:, 0, :], ACT.Ln).then_inc(lnv_ready[k], 1)
                act.wait_ge(lnv_ready[k], b + 1)
                nc.scalar.activation(small[:, 2, :], small[:, 1, :], ACT.Exp, scale=-0.5).then_inc(y0_ready[k], 1)

            def modulate(b, k):
                count = value(act, b + 1)
                act.wait_ge(mod_step, MOD_STEPS)
                act.wait_ge(read[f"rstd{k}"], count)
                nc.scalar.activation(hT[:, :], xc, ACT.Identity, scale=mod[:, 3 * k + 1, ds(b, 1)],
                                     bias=mod[:, 3 * k, ds(b, 1)]).then_inc(h_ready[k], 1)

            def front(gap, b):
                par = b % 2
                if gap == 2:
                    square(b, 0)
                if gap == 4:
                    rsqrt_seed(b, 0)
                if gap == 7:
                    modulate(b, 0)
                if gap in (9, 11):
                    a = gap // 2 - 4
                    act.wait_ge(filled[f"u{a}"], b + 1)
                    nc.scalar.activation(ub[:, a, CONVK - 1:], PF, ACT.Identity, bias=cols[:, 0, a:a + 1]
                                         ).then_inc(read[f"u{a}"], 1)
                if gap in (11, 13):
                    a = gap // 2 - 5
                    act.wait_ge(pad_clear, b + 1)
                    act.wait_ge(read[f"u{a}"], b + 1)
                    wait(act, filled["wo"], b - 1)
                    nc.scalar.activation(z[:, a, :], ub[:, a, 0:SEQ], ACT.Identity, scale=conv[:, a, 0:1],
                                         bias=cols[:, 2, a:a + 1]).then_inc(conv_step[a], 1)
                if gap in (13, 15):
                    a = gap // 2 - 6
                    count = value(act, b + 1)
                    act.wait_ge(mod_step, MOD_STEPS)
                    act.wait_ge(filled[f"gate{a}"], count)
                    nc.scalar.activation(gate[:, ds(par, 1), a, :], PF.unsqueeze(1), ACT.Tanh, scale=0.5,
                                         bias=b2half[:, a:a + 1]).then_inc(read[f"gate{a}"], 1)
                if gap == 17:
                    for a in range(HALVES):
                        act.wait_ge(conv_step[a], (b + 1) * CONVK)
                    nc.scalar.activation(u[:, :, :], z[:, :, :], ACT.Tanh, scale=0.5).then_inc(tanhz_ready, 1)
                if gap == 18:
                    act.wait_ge(tanhz_ready, b + 1)
                    nc.scalar.activation(u[:, :, :], u[:, :, :], ACT.Identity, scale=0.5, bias=half[:, 0:1]
                                         ).then_inc(u_ready, 1)
                if gap == 20:
                    act.wait_ge(filled["xproj"], b + 1)
                    nc.scalar.copy(xdt[:, :], PF[0:DTRANK, :]).then_inc(read["xproj"], 1)
                if gap in (22, 24):
                    a = gap // 2 - 11
                    act.wait_ge(filled[f"dt{a}"], b + 1)
                    nc.scalar.activation(v_sb[:, a, :], PF, ACT.Identity, bias=cols[:, 3, a:a + 1]
                                         ).then_inc(read[f"dt{a}"], 1)
                if gap == 25:
                    for a in range(HALVES):
                        act.wait_ge(read[f"dt{a}"], b + 1)
                    nc.scalar.activation(e_sb, v_sb[:, :, :], ACT.Abs).then_inc(av_ready, 1)
                if gap == 26:
                    act.wait_ge(av_ready, b + 1)
                    nc.scalar.activation(e_sb, e_sb, ACT.Exp, scale=-1.0).then_inc(e_ready, 1)
                    act.wait_ge(e_ready, b + 1)
                    nc.scalar.activation(w_sb, e_sb, ACT.Identity, bias=1.0).then_inc(w_ready, 1)
                if gap == 27:
                    act.wait_ge(w_ready, b + 1)
                    nc.scalar.activation(lw_sb[:, :, :], w_sb, ACT.Ln).then_inc(lw_ready, 1)

            def tail(gap, b):
                if gap == 3:
                    act.wait_ge(summed, NSTATE * (b + 1))
                    nc.scalar.copy(ysb[:, :, :].rearrange("p c m -> p (c m)"), PY).then_inc(y_out, 1)
                if gap == 9:
                    count = value(act, b + 1)
                    act.wait_ge(mod_step, MOD_STEPS)
                    act.wait_ge(filled["wo"], count)
                    nc.scalar.activation(o_sb, PF, ACT.Identity, scale=gahalf[:, ds(b, 1)], bias=gabo[:, ds(b, 1)]
                                         ).then_inc(read["wo"], 1)
                if gap == 12:
                    square(b, 1)
                if gap == 14:
                    rsqrt_seed(b, 1)
                if gap == 16:
                    modulate(b, 1)
                if gap == 18:
                    act.wait_ge(route, b * 12 + 2)
                    nc.scalar.activation(prob[:, :], prob[:, :], ACT.Exp).then_inc(prob_exp, 1)
                if gap == 19:
                    act.wait_ge(filled["rows"], b + 1)
                    act.wait_ge(table_cleared, 16 * BATCH)
                    scattered_before(act, b)
                    nc.scalar.copy(h2r[:, :, :].rearrange("p c h -> p (c h)"), PF).then_inc(read["rows"], 1)

            def gap_work(gap, tail_b, front_b):
                if front_b is not None:
                    front(gap, front_b)
                if tail_b is not None:
                    tail(gap, tail_b)

            def decays(b, n):
                for a in range(HALVES):
                    free = value(act, (b * NSTATE + n) * HALVES + a - DA_SLOTS + 1)
                    row = value(act, b + 1)
                    act.wait_ge(mod_step, MOD_STEPS)
                    if n == 0:
                        act.wait_ge(delta_ready, row)
                    wait(act, scanned, free)
                    nc.scalar.activation(dA[:, (n * HALVES + a) % DA_SLOTS, :].unsqueeze(1),
                                         dd[:, ds(b % 2, 1), 0, a, :], ACT.Exp,
                                         scale=A[:, a, n:n + 1]).then_inc(da_ready, 1)

            def scan(b, tail_b, front_b):
                for n in range(NSTATE):
                    step = b * NSTATE + n
                    wait_product(act, b, n - C_SLOTS)
                    for g in range(SEG):
                        act.wait_ge(c_filled, step * SEG + g + 1)
                        nc.scalar.copy(Csb[:, n % C_SLOTS, g * BANK:(g + 1) * BANK], PBC[g]).then_inc(c_copied, 1)
                    gap_work(2 * n, tail_b, front_b)
                    if n + 1 < NSTATE:
                        decays(b, n + 1)
                    elif front_b is not None:
                        decays(front_b, 0)
                    gap_work(2 * n + 1, tail_b, front_b)

            act.wait_ge(loaded["c"], 48)
            nc.scalar.activation(siluc[:, :], cT[:, :], ACT.Silu).then_inc(siluc_ready, 1)
            act.wait_ge(loaded["attn"], 16 * ATTN_LOADS)
            nc.scalar.activation(A[:, :, :], A[:, :, :], ACT.Exp).then_inc(a_exp, 1)
            act.wait_ge(mod_step, MOD_STEPS)
            each_gap(0, front)
            decays(0, 0)
            rows(lambda b: scan(b, None, b + 1), lambda b: scan(b, b - 1, b + 1), lambda b: scan(b, b - 1, None), act)
            for gap in range(TAIL_GAP):
                tail(gap, BATCH - 1)

            def tile(k, par, rnd):
                static = isinstance(k, int)
                if not static or k < TILES:
                    act.wait_ge(g_filled, k + 1)
                    wait(act, sg_ready, k - 1)
                    nc.scalar.activation(th[:, par % 2, :], PG(par)[:, 0:INTER], ACT.Tanh, scale=0.5
                                         ).then_inc(tanh_ready, 1)
                if not static or 0 <= k - 1 < TILES:
                    act.wait_ge(it_filled, k)
                    wait(act, o_filled, k - 2)
                    nc.scalar.copy(innerT[:, (par - 1) % 2, :], PI[:, 0:NIN * P]).then_inc(it_read, 1)

            def send(b):
                act.wait_ge(mt_read, (b + 1) * SEG)
                act.dma_start(outT_d[:, b * SEQ:(b + 1) * SEQ], xT[:, b * SEQ:(b + 1) * SEQ]).then_inc(stored, 16)

            tile_schedule(act, tile, tail, lambda: None, lambda b: send(b - 1) if b else None)
            send(BATCH - 1)
            act.wait_ge(stored, 16 * BATCH)

        @block.vector
        def _(dve):
            V = nc.vector

            def center(b, k):
                dve.wait_ge(filled[f"mean{k}"], b + 1)
                V.tensor_tensor(xc, xT[:, ds(b * SEQ, SEQ)], PF, ALU.subtract).then_inc(read[f"mean{k}"], 1)

            def variance(b, k):
                dve.wait_ge(filled[f"var{k}"], b + 1)
                V.tensor_scalar(small[:, 0, :], PF[:, 0:CH], LN_EPS, None, ALU.add).then_inc(read[f"var{k}"], 1)

            def rsqrt(b, k):
                dve.wait_ge(y0_ready[k], b + 1)
                V.tensor_tensor(small[:, 3, :], small[:, 0, :], small[:, 2, :], ALU.mult).then_inc(newton[k], 1)
                dve.wait_ge(newton[k], b * 3 + 1)
                V.tensor_tensor(small[:, 4, :], small[:, 3, :], small[:, 2, :], ALU.mult).then_inc(newton[k], 1)
                dve.wait_ge(newton[k], b * 3 + 2)
                V.tensor_scalar(small[:, 3, :], small[:, 4, :], -0.5, 1.5, ALU.mult, ALU.add).then_inc(newton[k], 1)
                dve.wait_ge(newton[k], b * 3 + 3)
                V.tensor_tensor(small[:, 5, :], small[:, 3, :], small[:, 2, :], ALU.mult).then_inc(rstd_ready[k], 1)

            def normalise(b, k):
                dve.wait_ge(filled[f"rstd{k}"], b + 1)
                V.tensor_tensor(xc, xc, PF, ALU.mult).then_inc(read[f"rstd{k}"], 1)

            def tap(b, a, k):
                dve.wait_ge(conv_step[a], b * CONVK + k)
                V.scalar_tensor_tensor(z[:, a, :], ub[:, a, k:k + SEQ], conv[:, a, k:k + 1], z[:, a, :],
                                       ALU.mult, ALU.add).then_inc(conv_step[a], 1)

            def front(gap, b):
                par = b % 2
                if gap == 2:
                    center(b, 0)
                if gap == 4:
                    variance(b, 0)
                if gap == 6:
                    rsqrt(b, 0)
                if gap == 7:
                    normalise(b, 0)
                if gap == 8:
                    V.memset(ubpad, 0.0).then_inc(pad_clear, 1)
                if gap == 13:
                    tap(b, 0, 1)
                    tap(b, 0, 2)
                if gap == 14:
                    tap(b, 1, 1)
                    tap(b, 0, 3)
                if gap in (15, 16):
                    tap(b, 1, gap - 13)
                if gap == 20:
                    rows_in = PF[DTRANK:PROJ, :].unsqueeze(1)
                    dve.wait_ge(filled["xproj"], b + 1)
                    V.tensor_copy(bcs[0:2 * NSTATE, ds(par, 1), :], rows_in).then_inc(read["xproj"], 1)
                    dve.wait_ge(read["xproj"], b * 3 + 2)
                    V.tensor_tensor(bcs[2 * NSTATE:4 * NSTATE, ds(par, 1), :], rows_in,
                                    bcs[0:2 * NSTATE, ds(par, 1), :].bitcast(fp32), ALU.subtract
                                    ).then_inc(read["xproj"], 1)
                if gap == 28:
                    dve.wait_ge(w_ready, b + 1)
                    V.scalar_tensor_tensor(e_sb, w_sb, 1.0, e_sb, ALU.subtract, ALU.subtract).then_inc(lost_ready, 1)
                    dve.wait_ge(lost_ready, b + 1)
                    V.scalar_tensor_tensor(v_sb[:, :, :], v_sb[:, :, :], 0.0, e_sb, ALU.max, ALU.subtract
                                           ).then_inc(softplus_step, 1)
                if gap == 29:
                    dve.wait_ge(lw_ready, b + 1)
                    V.scalar_tensor_tensor(lw_sb[:, :, :], w_sb, 1.0, lw_sb[:, :, :], ALU.is_gt, ALU.mult
                                           ).then_inc(softplus_step, 1)
                if gap == 30:
                    delta = dd[:, ds(par, 1), 0].squeeze(1)
                    dve.wait_ge(softplus_step, b * 2 + 2)
                    V.tensor_tensor(delta, v_sb[:, :, :], lw_sb[:, :, :], ALU.add).then_inc(delta_ready, 1)
                if gap == 31:
                    delta, du = (dd[:, ds(par, 1), i].squeeze(1) for i in range(2))
                    dve.wait_ge(delta_ready, b + 1)
                    V.tensor_tensor(du, delta, u[:, :, :], ALU.mult).then_inc(du_ready, 1)

            def per_chunk(v):
                return v.unsqueeze(2).to_broadcast([P, CH, EXPERTS])

            def by_expert(v, n=CH):
                return v.rearrange("p (c e) -> p c e", e=EXPERTS)

            def tail(gap, b):
                step = [b * 12]

                def then(ins):
                    ins.then_inc(route, 1)
                    step[0] = step[0] + 1
                    dve.wait_ge(route, step[0])

                if gap in (5, 6):
                    a = gap - 5
                    dve.wait_ge(filled[f"yT{a}"], b + 1)
                    V.scalar_tensor_tensor(yg[:, a, :].unsqueeze(1), gate[:, ds(b % 2, 1), a, :], 1.0, PF.unsqueeze(1),
                                           ALU.add, ALU.mult).then_inc(read[f"yT{a}"], 1)
                if gap == 11:
                    dve.wait_ge(read["wo"], b + 1)
                    V.tensor_tensor(xT[:, ds(b * SEQ, SEQ)], xT[:, ds(b * SEQ, SEQ)], o_sb, ALU.add).then_inc(x1_ready, 1)
                if gap == 12:
                    center(b, 1)
                if gap == 14:
                    variance(b, 1)
                if gap == 15:
                    rsqrt(b, 1)
                if gap == 16:
                    normalise(b, 1)
                if gap == 18:
                    dve.wait_ge(filled["logit"], b + 1)
                    then(V.tensor_copy(prob[:, :], PF[:, 0:RW]))
                    V.reduce_max(stat[:, 0, :], by_expert(prob[:, :]), AX.X).then_inc(read["logit"], 1)
                    dve.wait_ge(read["logit"], b + 1)
                    V.tensor_tensor(by_expert(prob[:, :]), by_expert(prob[:, :]), per_chunk(stat[:, 0, :]),
                                    ALU.subtract).then_inc(route, 1)
                if gap == 19:
                    step[0] = b * 12 + 2
                    dve.wait_ge(prob_exp, b + 1)
                    then(V.reduce_sum(stat[:, 0, :], by_expert(prob[:, :]), AX.X))
                    then(V.reciprocal(stat[:, 1, :], stat[:, 0, :]))
                    then(V.tensor_tensor(by_expert(prob[:, :]), by_expert(prob[:, :]), per_chunk(stat[:, 1, :]), ALU.mult))
                    shape = [P, CH, EXPERTS, EXPERTS]
                    p3 = by_expert(prob[:, :])
                    other, own = p3.unsqueeze(2).to_broadcast(shape), p3.unsqueeze(3).to_broadcast(shape)
                    ah, ti = (t[:, :].rearrange("p (c e f) -> p c e f", c=CH, e=EXPERTS) for t in (ahead, ties))
                    then(V.tensor_tensor(ti, other, own, ALU.is_equal))
                    then(V.tensor_tensor(ti, ti, before[:, :, :].unsqueeze(1).to_broadcast(shape), ALU.mult))
                    then(V.tensor_tensor(ah, other, own, ALU.is_gt))
                    then(V.tensor_tensor(ahead[:, :], ahead[:, :], ties[:, :], ALU.add))
                    then(V.reduce_sum(by_expert(rank[:, :]), ah, AX.X))
                    V.tensor_scalar(chosen[:, 0, :], rank[:, :], 0.0, None, ALU.is_equal).then_inc(route, 1)
                    V.tensor_scalar(chosen[:, 1, :], rank[:, :], 1.0, None, ALU.is_equal).then_inc(route, 1)
                    V.tensor_scalar(both[:, :], rank[:, :], TOPK - 0.5, None, ALU.is_lt).then_inc(chosen_ready, 1)
                if gap == 21:
                    dve.wait_ge(route, b * 12 + 12)
                    V.scalar_tensor_tensor(picked[:, :, :], chosen[:, :, :], 0.5,
                                           prob[:, :].unsqueeze(1).to_broadcast([P, TOPK, RW]), ALU.mult, ALU.mult
                                           ).then_inc(wsum, 1)
                    dve.wait_ge(wsum, b + 1)
                    V.reduce_sum(wsel[:, ds(b, 1), :].rearrange("p b (j c) -> p (b j) c", c=CH),
                                 picked[:, :, :].rearrange("p j (c e) -> p j c e", e=EXPERTS), AX.X).then_inc(wsel_ready, 1)
                if gap == 23:
                    positions(b)

            def positions(b):
                s = [b * 14]

                def then(ins):
                    ins.then_inc(place, 1)
                    s[0] = s[0] + 1
                    dve.wait_ge(place, s[0])

                dve.wait_ge(filled["prefix"], b + 1)
                V.tensor_copy(by_expert(slot_f[:, :]), by_expert(PF[:, 0:RW])).then_inc(read["prefix"], 1)
                V.tensor_copy(sums[:, 0, HEAD:, :], by_expert(PF[:, BANK:BANK + RW])).then_inc(read["prefix"], 1)
                dve.wait_ge(read["prefix"], 2 * (b + 1))
                for i, shift in enumerate((1, 2, 4)):
                    then(V.tensor_tensor(sums[:, (i + 1) % 2, HEAD:, :], sums[:, i % 2, HEAD:, :],
                                         sums[:, i % 2, HEAD - shift:HEAD - shift + CH, :], ALU.add))
                total = sums[:, 1, HEAD + CH - 1, :]
                then(V.tensor_scalar(ntile_i[:, :], total, float(P - 1), None, ALU.add))
                then(V.tensor_scalar(ntile_i[:, :], ntile_i[:, :], 7, None, ALU.arith_shift_right))
                then(V.tensor_copy(ntile[:, :], ntile_i[:, :]))
                then(V.tensor_tensor(pairs8[:, :, :], before[:, :, :],
                                     ntile[:, :].unsqueeze(1).to_broadcast([P, EXPERTS, EXPERTS]), ALU.mult))
                then(V.reduce_sum(starts[:, :], pairs8[:, :, :], AX.X))
                then(V.tensor_tensor(ends[:, :], starts[:, :], ntile[:, :], ALU.add))
                then(V.tensor_scalar(starts[:, :], starts[:, :], float(P), rowbase[:, 0:1], ALU.mult, ALU.add))
                then(V.tensor_tensor(by_expert(slot_f[:, :]), by_expert(slot_f[:, :]),
                                     sums[:, 1, HEAD - 1:HEAD - 1 + CH, :], ALU.add))
                then(V.tensor_tensor(by_expert(slot_f[:, :]), by_expert(slot_f[:, :]),
                                     starts[:, :].unsqueeze(1).to_broadcast([P, CH, EXPERTS]), ALU.add))
                then(V.tensor_tensor(picked[:, :, :], chosen[:, :, :],
                                     slot_f[:, :].unsqueeze(1).to_broadcast([P, TOPK, RW]), ALU.mult))
                then(V.reduce_sum(pos_f[:, :].rearrange("p (j c) -> p j c", j=TOPK),
                                  picked[:, :, :].rearrange("p j (c e) -> p j c e", e=EXPERTS), AX.X))
                scattered_before(dve, b)
                V.tensor_copy(pos[:, :], pos_f[:, :]).then_inc(pos_ready, 1)
                V.tensor_copy(pos_all[:, ds(b, 1), :].squeeze(1), pos_f[:, :]).then_inc(rowstep, 1)
                shape = [P, ROW_TILES, EXPERTS]
                pt = past[:, :].rearrange("p (k e) -> p k e", e=EXPERTS)
                V.tensor_tensor(pt, tile_f[:, :].unsqueeze(2).to_broadcast(shape),
                                ends[:, :].unsqueeze(1).to_broadcast(shape), ALU.is_ge).then_inc(table, 1)
                dve.wait_ge(table, b * 4 + 1)
                V.reduce_sum(expert_f[:, :], pt, AX.X).then_inc(table, 1)
                if isinstance(b, int) and b == BATCH - 2:
                    V.memset(rowbase[:, :], 0.0).then_inc(table, 1)
                else:
                    V.tensor_scalar(rowbase[:, :], rowbase[:, :], float(ROW_SLOTS), None, ALU.add).then_inc(table, 1)
                dve.wait_ge(table, b * 4 + 3)
                V.tensor_scalar(expert[:, ds(b * ROW_TILES, ROW_TILES)], expert_f[:, :], float(EXPERTS - 1), None, ALU.min
                                ).then_inc(table, 1)

            def gap_work(gap, tail_b, front_b):
                if front_b is not None:
                    front(gap, front_b)
                if tail_b is not None:
                    tail(gap, tail_b)

            def scan(b, tail_b, front_b):
                dve.wait_ge(du_ready, b + 1)
                for n in range(NSTATE):
                    step = b * NSTATE + n
                    wait(dve, summed, step - RING + 1)
                    for g in range(SEG):
                        cut = slice(g * BANK, (g + 1) * BANK)
                        dve.wait_ge(b_filled, step * SEG + g + 1)
                        V.tensor_tensor(ring[:, n % RING, :, cut], dd[:, ds(b % 2, 1), 1, :, cut].squeeze(1),
                                        PBC[g].unsqueeze(1).to_broadcast([P, HALVES, BANK]), ALU.mult
                                        ).then_inc(dbu_ready, 1)
                    gap_work(2 * n, tail_b, front_b)
                    dve.wait_ge(dbu_ready, (step + 1) * SEG)
                    for a in range(HALVES):
                        dve.wait_ge(da_ready, step * HALVES + a + 1)
                        V.tensor_tensor_scan(ring[:, n % RING, a, :], dA[:, (n * HALVES + a) % DA_SLOTS, :],
                                             ring[:, n % RING, a, :], 0.0, ALU.mult, ALU.add).then_inc(scanned, 1)
                    if on_dve(b, n):
                        dve.wait_ge(scanned, (step + 1) * HALVES)
                        dve.wait_ge(c_copied, (step + 1) * SEG)
                        V.tensor_tensor(ring[:, n % RING], ring[:, n % RING],
                                        Csb[:, n % C_SLOTS, :].unsqueeze(1).to_broadcast([P, HALVES, SEQ]), ALU.mult
                                        ).then_inc(dve_prod_ready, 1)
                    gap_work(2 * n + 1, tail_b, front_b)

            V.memset(mean_w[:, :], 1.0 / HID).then_inc(mod_step, 1)
            V.memset(sums[:, :, :, :], 0.0).then_inc(mod_step, 1)
            V.memset(rowbase[:, :], 0.0).then_inc(mod_step, 1)
            V.memset(half[:, :], 0.5).then_inc(mod_step, 1)
            dve.wait_ge(setup, SETUP)
            V.tensor_tensor(pick[:, :], ident[0:4 * NSTATE, 0:2 * NSTATE], ident[0:4 * NSTATE, 2 * NSTATE:4 * NSTATE],
                            ALU.add).then_inc(mod_step, 1)
            V.tensor_copy(tile_f[:, :], tile_i[:, :]).then_inc(mod_step, 1)
            dve.wait_ge(mod_filled, 1)
            V.tensor_copy(mod[:, :, :], PBC[0][:, 0:6 * BATCH].rearrange("p (k b) -> p k b", k=6)).then_inc(mod_step, 1)
            dve.wait_ge(mod_step, 7)
            gates = mod[:, 2:6:3, :]
            V.tensor_scalar(modt[:, :, :], gates, -1.0, 0.25, ALU.mult, ALU.max).then_inc(mod_step, 1)
            dve.wait_ge(mod_step, 8)
            V.tensor_tensor(modt[:, :, :], modt[:, :, :], gates, ALU.max).then_inc(mod_step, 1)
            V.tensor_scalar(mod[:, 1:5:3, :], mod[:, 1:5:3, :], 1.0, None, ALU.add).then_inc(mod_step, 1)
            dve.wait_ge(mod_step, 10)
            V.tensor_scalar(gates, gates, 0.0, 2.0, ALU.is_ge, ALU.mult).then_inc(mod_step, 1)
            dve.wait_ge(mod_step, 11)
            V.scalar_tensor_tensor(gates, gates, -1.0, modt[:, :, :], ALU.add, ALU.mult).then_inc(mod_step, 1)
            dve.wait_ge(mod_step, 12)
            V.tensor_scalar(gabo[:, :], mod[:, 2, :], bo[:, 0:1], None, ALU.mult).then_inc(mod_step, 1)
            V.tensor_scalar(gahalf[:, :], mod[:, 2, :], 0.5, None, ALU.mult).then_inc(mod_step, 1)
            dve.wait_ge(loaded["attn"], 16 * ATTN_LOADS)
            for a in range(HALVES):
                V.tensor_scalar(Ddiag[:, a, :], ident[:, :], cols[:, 4, a:a + 1], None, ALU.mult).then_inc(mod_step, 1)
            V.tensor_scalar(b2half[:, :], cols[:, 1, :], 0.5, None, ALU.mult).then_inc(mod_step, 1)
            dve.wait_ge(a_exp, 1)
            V.tensor_scalar(A[:, :, :], A[:, :, :], -1.0, None, ALU.mult).then_inc(mod_step, 1)
            dve.wait_ge(mod_step, MOD_STEPS)

            each_gap(0, front)
            rows(lambda b: scan(b, None, b + 1), lambda b: scan(b, b - 1, b + 1), lambda b: scan(b, b - 1, None), dve)

            def turned(k, par):
                dve.wait_ge(xt_filled, k + 1)
                wait(dve, u_filled, k - 1)
                V.tensor_copy(xsT[:, par % 2, :], PX).then_inc(xt_read, 1)

            def tile(k, par, rnd):
                static = isinstance(k, int)
                if not static or k + 1 < TILES:
                    turned(k + 1, par + 1)
                if not static or 0 <= k - 3 < TILES:
                    slot = (par - 3) % XS_SLOTS
                    dve.wait_ge(o_filled, k - 2)
                    wait(dve, ys_stored[slot], 16 * (rnd + (-1 if par < 3 else 0)))
                    V.tensor_copy(ob[:, slot, :], PO).then_inc(o_read, 1)
                if not static or k < TILES:
                    dve.wait_ge(tanh_ready, k + 1)
                    wait(dve, inner_ready, k - 1)
                    V.scalar_tensor_tensor(sg[:, par % 2, :], th[:, par % 2, :], 1.0, PG(par)[:, 0:INTER], ALU.add, ALU.mult
                                           ).then_inc(sg_ready, 1)
                    dve.wait_ge(sg_ready, k + 1)
                    dve.wait_ge(u_filled, k + 1)
                    wait(dve, it_filled, k - 1)
                    V.tensor_tensor(inner[:, par % 2, :], sg[:, par % 2, :], PU[:, 0:INTER], ALU.mult).then_inc(inner_ready, 1)

            def combine(b):
                wait(dve, mt_filled, b * SEG)
                m0 = b * TOPK * CH
                for c in range(CH):
                    dve.wait_ge(gathered[c], 16 * TOPK * (b + 1))
                    V.tensor_scalar(mix[:, c, :], gath[:, 0, c, :], wsel[:, ds(b, 1), c:c + 1].squeeze(1), None, ALU.mult
                                    ).then_inc(mixed, 1)
                    dve.wait_ge(mixed, m0 + 2 * c + 1)
                    V.scalar_tensor_tensor(mix[:, c, :], gath[:, 0, CH + c, :], wsel[:, ds(b, 1), CH + c:CH + c + 1].squeeze(1),
                                           mix[:, c, :], ALU.mult, ALU.add).then_inc(mixed, 1)
                for g in range(SEG):
                    cut = ds(b * SEQ + g * BANK, BANK)
                    dve.wait_ge(mt_filled, b * SEG + g + 1)
                    V.scalar_tensor_tensor(xT[:, cut], PM, mod[:, 5, ds(b, 1)], xT[:, cut], ALU.mult, ALU.add
                                           ).then_inc(mt_read, 1)
                if b + 1 < BATCH:
                    V.tensor_scalar(pos_g[:, :], pos_all[:, b + 1, :], float(-((b + 1) % (BATCH - 1)) * ROW_SLOTS), None, ALU.add
                                    ).then_inc(pos_back, 1)

            turned(0, 0)
            tile_schedule(dve, tile, tail, lambda: V.tensor_copy(pos_g[:, :], pos_all[:, 0, :]).then_inc(pos_back, 1),
                          combine)


def kernel(**inputs):
    import numpy as np
    import concourse.bacc as bacc
    from concourse import mybir as mb
    from concourse.bass_utils import run_bass_kernel_spmd

    a = {k: np.asarray(v) for k, v in inputs.items()}
    at, ff = "L0_attn_", "L0_ffn_"
    columns = np.stack([a[at + k].reshape(HALVES, P) for k in ("b1", "b2", "conv_b", "dt_proj_b", "D_skip")])
    arrays = {
        "xT": a[at + "x"].reshape(NTOK, HID).T,
        "w1": a[at + "W1"], "w2": a[at + "W2"], "wo": a[at + "Wo"],
        "xproj": a[at + "x_proj_w"], "dtw": a[at + "dt_proj_w"], "alog": a[at + "A_log"], "conv": a[at + "conv_w"],
        "cols": columns.transpose(2, 0, 1).reshape(P, 5 * HALVES), "bo": a[at + "bo"].reshape(P, 1),
        "router": a[ff + "router_w"].T,
        "gate": a[ff + "gate_w"].reshape(EXPERTS * INTER, HID).T,
        "up": a[ff + "up_w"].reshape(EXPERTS * INTER, HID).T,
        "down": a[ff + "down_w"].transpose(0, 2, 1).reshape(EXPERTS * INTER, HID),
        "cT": a["L0_c"].T, "wmod": a["L0_wmod"],
    }
    arrays = {f"in_{k}": np.ascontiguousarray(v) for k, v in arrays.items()}
    nc = bacc.Bacc("TRN2", target_bir_lowering=False, num_devices=1)
    args = [nc.dram_tensor(k, v.shape, mb.dt.from_np(v.dtype), kind="ExternalInput").ap() for k, v in arrays.items()]
    out = nc.dram_tensor("out_T", (HID, NTOK), mb.dt.float32, kind="ExternalOutput").ap()
    token_tables = [nc.dram_tensor(f"token_table{k}", (n * ROW_SLOTS, HID), mb.dt.float32, kind="Internal").ap()
                    for k, n in enumerate((BATCH - 1, 1))]
    result_tables = [nc.dram_tensor(f"result_table{b}", (ROW_SLOTS, HID), mb.dt.float32, kind="Internal").ap()
                     for b in range(BATCH)]
    adaln_kernel(nc, *args, out, token_tables, result_tables)
    r = run_bass_kernel_spmd(nc, [arrays], core_ids=[0])
    return np.ascontiguousarray(np.asarray(r.results[0]["out_T"]).T).reshape(BATCH, SEQ, HID)
```

```python
from contextlib import ExitStack

import concourse.bass as bass
from concourse import mybir

fp32 = mybir.dt.float32
fp32r = mybir.dt.float32r
int32 = mybir.dt.int32
ALU = mybir.AluOpType
ACT = mybir.ActivationFunctionType
AX = mybir.AxisListType
ds = bass.ds

P = 128
BATCH, SEQ, HID = 4, 1024, 128
MLP, NSTATE, DTRANK, CONVK = 256, 16, 64, 4
EXPERTS, INTER, TOPK = 8, 352, 2
NTOK = BATCH * SEQ
HALVES = MLP // P
BANK = 512
CH = SEQ // P
SEG = SEQ // BANK
LN_EPS = 1e-5
PROJ = DTRANK + 2 * NSTATE
GAPS = 2 * NSTATE
RING, DA_SLOTS, C_SLOTS = 4, 4, 2

INNER = [(c * P, min(P, INTER - c * P)) for c in range(-(-INTER // P))]
NIN = len(INNER)
XS_SLOTS = 4
SHARED = BATCH - 1


def tiles_for(rows):
    return rows * TOPK * SEQ // P + EXPERTS - 1


SHARED_TILES, LAST_TILES = -(-tiles_for(SHARED) // XS_SLOTS) * XS_SLOTS, tiles_for(1)
TILES = SHARED_TILES + LAST_TILES
REGION = SHARED * SEQ + P
SPARE_TILES = SHARED_TILES - SHARED * TOPK * SEQ // P
MIX_STEP = SHARED_TILES + 6
TAIL_GAP = 4
DVE_PRODUCTS = (10, 12, 13, 14, 15)


def wait(eng, signal, count):
    if not (isinstance(count, int) and count <= 0):
        eng.wait_ge(signal, count)


def value(eng, count):
    return count if isinstance(count, int) else eng.snap(eng.to_reg(count))


def adaln_kernel(nc, xT_d, w1_d, w2_d, wo_d, xproj_d, dtw_d, alog_d, conv_d, cols_d, bo_d, router_d,
                 gate_d, up_d, down_d, cT_d, wmod_d, outT_d, xs_d, ys_d):
    ctx = ExitStack()
    with ctx:
        def sb(name, shape, dt=fp32):
            return ctx.enter_context(nc.sbuf_tensor(name, shape, dt))

        def sem(name):
            return ctx.enter_context(nc.semaphore(name))

        xT = sb("xT", [P, NTOK])
        ident = sb("ident", [P, P])
        mean_w = sb("mean_w", [P, P])
        ones = sb("ones", [P, P])
        below = sb("below", [P, P])
        pick = sb("pick", [2 * 2 * NSTATE, 2 * NSTATE], fp32r)
        w1 = sb("w1", [P, MLP])
        w2 = sb("w2", [P, MLP])
        wo = sb("wo", [P, HALVES, HID])
        xproj = sb("xproj", [P, HALVES, PROJ])
        dtw = sb("dtw", [DTRANK, MLP])
        A = sb("A", [P, HALVES, NSTATE])
        conv = sb("conv", [P, HALVES, CONVK])
        cols = sb("cols", [P, 5, HALVES])
        b2half = sb("b2half", [P, HALVES])
        half = sb("half", [P, 1])
        bo = sb("bo", [P, 1])
        Ddiag = sb("Ddiag", [P, HALVES, P])
        router = sb("router", [P, EXPERTS])
        cT = sb("cT", [P, BATCH])
        siluc = sb("siluc", [P, BATCH])
        mod = sb("mod", [P, 6, BATCH])
        modt = sb("modt", [P, 2, BATCH])
        gabo = sb("gabo", [P, BATCH])
        gahalf = sb("gahalf", [P, BATCH])
        before = sb("before", [P, EXPERTS, EXPERTS])
        tile_i = sb("tile_i", [P, SHARED_TILES], int32)
        tile_f = sb("tile_f", [P, SHARED_TILES])
        lane_i = sb("lane_i", [P, 1], int32)
        lane_f = sb("lane_f", [P, 1])
        region_f = sb("region_f", [P, EXPERTS])
        zeros = sb("zeros", [P, HID])
        xcsq = sb("xcsq", [P, 2, SEQ])
        xc, sq = xcsq[:, 0, :], xcsq[:, 1, :]
        hT = sb("hT", [P, SEQ])
        h2r = sb("h2r", [P, CH, HID])
        PADW = SEQ + P
        ubm = sb("ubm", [P, HALVES * PADW])
        z = sb("z", [P, HALVES, SEQ])
        ROWW = HALVES * SEQ
        stream = sb("stream", [P, ROWW + 2 * 2 * ROWW])
        u = stream[:, 0:ROWW].rearrange("p (a s) -> p a s", a=HALVES)
        dd = stream[:, ROWW:].rearrange("p (r k a s) -> p r k a s", r=2, k=2, a=HALVES)
        gate = sb("gate", [P, 2, HALVES, SEQ])
        xdt = sb("xdt", [DTRANK, SEQ])
        bcs = sb("bcs", [2 * 2 * NSTATE, 2, SEQ], fp32r)
        ysb = sb("ysb", [P, CH, MLP])
        Csb = sb("Csb", [P, C_SLOTS, SEQ])
        dA = sb("dA", [P, DA_SLOTS, SEQ])
        ring = sb("ring", [P, RING, HALVES, SEQ])
        small = sb("small", [P, 6, CH])
        RW = CH * EXPERTS
        prob = sb("prob", [P, RW])
        stat = sb("stat", [P, 2, CH])
        ahead = sb("ahead", [P, RW * EXPERTS])
        ties = sb("ties", [P, RW * EXPERTS])
        rank = sb("rank", [P, RW])
        chosen = sb("chosen", [P, TOPK, RW])
        both = sb("both", [P, RW])
        picked = sb("picked", [P, TOPK, RW])
        HEAD = CH // 2
        sums = sb("sums", [P, 2, HEAD + CH, EXPERTS])
        ntile_i = sb("ntile_i", [P, EXPERTS], int32)
        ntile = sb("ntile", [P, EXPERTS])
        firsts = sb("firsts", [P, EXPERTS])
        starts = sb("starts", [P, EXPERTS])
        ends = sb("ends", [P, EXPERTS])
        pairs8 = sb("pairs8", [P, EXPERTS, EXPERTS])
        slot_f = sb("slot_f", [P, RW])
        pos_f = sb("pos_f", [P, TOPK * CH])
        pos = sb("pos", [P, TOPK * CH], int32)
        pos_all = sb("pos_all", [P, SHARED * TOPK * CH])
        pos_g = sb("pos_g", [P, BATCH * TOPK * CH], int32)
        free = sb("free", [P, EXPERTS])
        shift = sb("shift", [P, SHARED * TOPK * CH * EXPERTS])
        moved = sb("moved", [P, SHARED * TOPK * CH])
        pad = sb("pad", [P, EXPERTS], int32)
        tile_row = sb("tile_row", [P, SHARED_TILES], int32)
        wsel = sb("wsel", [P, BATCH, TOPK * CH])
        past = sb("past", [P, SHARED_TILES * EXPERTS])
        expert_f = sb("expert_f", [P, SHARED_TILES])
        expert = sb("expert", [P, TILES], int32)

        ubv = ubm[:, :].rearrange("p (a s) -> p a s", a=HALVES)
        ub, ubpad = ubv[:, :, P - CONVK + 1:], ubv[:, :, P - CONVK + 1:P]
        yg = z
        o_sb = sq
        v_sb = z
        e_sb = ubm[:, 0:HALVES * SEQ].rearrange("p (a s) -> p a s", a=HALVES)
        w_sb = ysb[:, :, :].rearrange("p c m -> p (c m)").rearrange("p (a s) -> p a s", a=HALVES)
        lw_sb = xcsq
        wmod = ring[:, 0, 0, 0:6 * P].rearrange("p (k m) -> p k m", k=6)
        gate_w = stream[:, 0:EXPERTS * INTER]
        up_w = stream[:, EXPERTS * INTER:2 * EXPERTS * INTER]
        down_w = dA[:, :, :].rearrange("p r s -> p (r s)")[:, 0:NIN * EXPERTS * HID].rearrange("p (c m) -> p c m", c=NIN)
        gath = gate[:, :, :, :].rearrange("p r a s -> p (r a s)").rearrange("p (q j h) -> p q j h", j=TOPK, h=HID)
        GATH_SLOTS = 2 * ROWW // (TOPK * HID)

        def tiles_of(area, at, count, width=P):
            return area[:, at:at + count * width].rearrange("p (k h) -> p k h", k=count)

        odd = stream[:, 3 * ROWW:]
        xs, xsT, ob = tiles_of(odd, 0, XS_SLOTS), tiles_of(odd, 4 * P, 2), tiles_of(odd, 6 * P, XS_SLOTS)
        innerT = tiles_of(odd, 10 * P, 2, NIN * P)
        th, sg, inner = (tiles_of(ubm, 2 * k * INTER, 2, INTER) for k in range(3))
        mix = xc.rearrange("p (c h) -> p c h", h=HID)

        psum = ctx.enter_context(nc.psum_tensor("psum", [P, 8 * BANK], fp32))

        def bank(i, n=1):
            return psum[:, i * BANK:(i + n) * BANK]

        PY = bank(0, 4)
        PYc = PY.rearrange("p (c m) -> p c m", c=CH)
        PBC = [bank(4), bank(5)]
        PF = bank(6, 2)
        PX, PU, PI, PO, PM = bank(0)[:, 0:P], bank(3), bank(4), bank(5)[:, 0:P], bank(7)

        def PG(k):
            return bank(1 + k % 2)

        PIECES = ["mean0", "var0", "rstd0", "yT0", "yT1", "wo", "u0", "u1", "mean1", "gate0", "gate1", "var1",
                  "rstd1", "logit", "rows", "xproj", "dt0", "dt1", "prefix"]
        filled = {n: sem(f"{n}_filled") for n in PIECES}
        read = {n: sem(f"{n}_read") for n in PIECES}
        READS = {"xproj": 3, "prefix": 2}

        loaded = {n: sem(f"load_{n}") for n in ("c", "attn", "gateup", "down")}
        loaded_x = [sem(f"loaded_x{b}") for b in range(BATCH)]
        zeroed = sem("zeroed")
        setup = sem("setup")
        siluc_ready, mod_filled, mod_step, a_exp = (sem(n) for n in ("siluc_ready", "mod_filled", "mod_step", "a_exp"))
        sq_ready = [sem(f"sq{k}_ready") for k in range(2)]
        lnv_ready = [sem(f"lnv{k}_ready") for k in range(2)]
        y0_ready = [sem(f"y0{k}_ready") for k in range(2)]
        newton = [sem(f"newton{k}") for k in range(2)]
        rstd_ready = [sem(f"rstd{k}_ready") for k in range(2)]
        h_ready = [sem(f"h{k}_ready") for k in range(2)]
        pad_clear, conv_step = sem("pad_clear"), [sem(f"conv_step{a}") for a in range(HALVES)]
        tanhz_ready, u_ready = sem("tanhz_ready"), sem("u_ready")
        av_ready, e_ready, lw_ready, w_ready, lost_ready, log_ready, softplus_step, delta_ready, du_ready = (
            sem(n) for n in ("av_ready", "e_ready", "lw_ready", "w_ready", "lost_ready", "log_ready", "softplus_step", "delta_ready",
                             "du_ready"))
        b_filled, dbu_ready, c_filled, c_copied, da_ready, scanned, prod_ready, dve_prod_ready, summed = (
            sem(n) for n in ("b_filled", "dbu_ready", "c_filled", "c_copied", "da_ready", "scanned", "prod_ready", "dve_prod_ready",
                             "summed"))
        y_out, x1_ready = sem("y_out"), sem("x1_ready")
        route, prob_exp, chosen_ready, pos_ready, pos_kept, table_written, table_cleared, rowstep, wsum, wsel_ready, place, table, group, padded = (
            sem(n) for n in ("route", "prob_exp", "chosen_ready", "pos_ready", "pos_kept", "table_written", "table_cleared", "rowstep",
                             "wsum", "wsel_ready", "place", "table", "group", "padded"))
        xs_loaded = [sem(f"xs_loaded{k}") for k in range(XS_SLOTS)]
        xt_filled, xt_read, g_filled, u_filled, tanh_ready, sg_ready, inner_ready, it_filled, it_read, o_filled, o_read = (
            sem(n) for n in ("xt_filled", "xt_read", "g_filled", "u_filled", "tanh_ready", "sg_ready", "inner_ready",
                             "it_filled", "it_read", "o_filled", "o_read"))
        ys_stored = [sem(f"ys_stored{k}") for k in range(XS_SLOTS)]
        gathered = [sem(f"gathered{k}") for k in range(GATH_SLOTS)]
        mixed, mt_filled, mt_read, stored = (
            sem(n) for n in ("mixed", "mt_filled", "mt_read", "stored"))

        ATTN_LOADS = 9
        SETUP = 9
        PAD_STEP, GROUP_STEPS = 1, 20
        MOD_STEPS = 20
        block = ctx.enter_context(nc.Block())

        def writes(b):
            return 16 * b * TOPK * CH

        def scattered_before(eng, b):
            if isinstance(b, int):
                wait(eng, table_written, writes(b))
            else:
                eng.wait_ge(prod_ready, (b + 1) * NSTATE + 1)

        def on_dve(b, n):
            return isinstance(b, int) and b == BATCH - 1 and n in DVE_PRODUCTS

        def wait_product(eng, b, n):
            if n < 0:
                b, n = b - 1, n + NSTATE
            if isinstance(b, int) and b < 0:
                return
            if on_dve(b, n):
                eng.wait_ge(dve_prod_ready, DVE_PRODUCTS.index(n) + 1)
            else:
                own = sum(on_dve(b, m) for m in range(n))
                eng.wait_ge(prod_ready, b * NSTATE + n + 1 - own)

        def each_gap(b, work):
            for gap in range(GAPS):
                work(gap, b)

        def rows(first, inside, last, eng):
            first(0)
            with eng.Fori(1, BATCH - 1) as b:
                inside(b)
            last(BATCH - 1)

        def tile_schedule(eng, tile, beside, combine):
            opening = -(-(GAPS - TAIL_GAP) // XS_SLOTS)
            closing = MIX_STEP // XS_SLOTS
            for t in range(opening * XS_SLOTS):
                beside(TAIL_GAP + t, BATCH - 1)
                tile(t, t % XS_SLOTS, t // XS_SLOTS)
            with eng.Fori(opening, closing) as i:
                for k in range(XS_SLOTS):
                    tile(i * XS_SLOTS + k, k, i)
            for t in range(closing * XS_SLOTS, MIX_STEP + BATCH * CH + 4):
                if t < TILES + 3:
                    rnd = min(t // XS_SLOTS, (TILES - 1) // XS_SLOTS)
                    tile(t, t - rnd * XS_SLOTS, rnd)
                if t >= MIX_STEP:
                    combine(t - MIX_STEP)

        @block.sync
        def _(sp):
            sp.dma_start(cT[:, :], cT_d).then_inc(loaded["c"], 16)
            sp.dma_start(wmod, wmod_d.rearrange("h (k m) -> h k m", k=6)).then_inc(loaded["c"], 16)
            sp.dma_start(bo[:, :], bo_d).then_inc(loaded["c"], 16)
            sp.dma_start(xT[:, 0:SEQ], xT_d[:, 0:SEQ]).then_inc(loaded_x[0], 16)
            sp.dma_start(w1[:, :], w1_d).then_inc(loaded["attn"], 16)
            sp.dma_start(w2[:, :], w2_d).then_inc(loaded["attn"], 16)
            sp.dma_start(wo[:, :, :], wo_d.rearrange("(a p) m -> p a m", p=P)).then_inc(loaded["attn"], 16)
            sp.dma_start(xproj[:, :, :], xproj_d.rearrange("(a p) m -> p a m", p=P)).then_inc(loaded["attn"], 16)
            sp.dma_start(dtw[:, :], dtw_d).then_inc(loaded["attn"], 16)
            sp.dma_start(A[:, :, :], alog_d.rearrange("(a p) m -> p a m", p=P)).then_inc(loaded["attn"], 16)
            sp.dma_start(conv[:, :, :], conv_d.rearrange("(a p) m -> p a m", p=P)).then_inc(loaded["attn"], 16)
            sp.dma_start(cols[:, :, :], cols_d.rearrange("p (k a) -> p k a", k=5)).then_inc(loaded["attn"], 16)
            sp.dma_start(router[:, :], router_d).then_inc(loaded["attn"], 16)
            for b in range(1, BATCH):
                sp.dma_start(xT[:, b * SEQ:(b + 1) * SEQ], xT_d[:, b * SEQ:(b + 1) * SEQ]).then_inc(loaded_x[b], 16)
            sp.wait_ge(zeroed, 1)
            for table_, first, n in ((xs_d[1], 0, LAST_TILES), (xs_d[0], EXPERTS * REGION, SPARE_TILES)):
                sp.dma_start(table_[first:first + n * P, :].rearrange("(k p) h -> p k h", p=P),
                             zeros[:, :].unsqueeze(1).to_broadcast([P, n, HID])).then_inc(table_cleared, 16)
            sp.wait_ge(summed, (BATCH - 1) * NSTATE + 1)
            sp.dma_start(gate_w, gate_d).then_inc(loaded["gateup"], 16)
            sp.dma_start(up_w, up_d).then_inc(loaded["gateup"], 16)
            sp.wait_ge(scanned, BATCH * NSTATE * HALVES)
            sp.wait_ge(table_written, writes(SHARED))
            sp.wait_ge(padded, 16 * EXPERTS)
            sp.wait_ge(group, GROUP_STEPS)
            rounds, shared_rounds = -(-TILES // XS_SLOTS), SHARED_TILES // XS_SLOTS

            def load(i, k, shared):
                t = i * XS_SLOTS + k
                row = (sp.value_load(tile_row[0:1, ds(t, 1)], min_val=0, max_val=EXPERTS * REGION + (SPARE_TILES - 1) * P)
                       if shared else (t - SHARED_TILES) * P)
                if not isinstance(i, int) or i > 0:
                    sp.wait_ge(xt_filled, t + (1 - XS_SLOTS))
                sp.dma_start(xs[:, k, :], xs_d[1 - shared][ds(row, P), :]).then_inc(xs_loaded[k], 16)

            for k in range(XS_SLOTS):
                load(0, k, True)
            for c, (i0, k) in enumerate(INNER):
                sp.dma_start(down_w[0:k, c, :].rearrange("i (e h) -> i e h", e=EXPERTS),
                             down_d.rearrange("(e i) h -> i e h", e=EXPERTS)[i0:i0 + k, :, :]).then_inc(loaded["down"], 16)

            def store(i, k, shared):
                t = i * XS_SLOTS + k
                sp.wait_ge(o_read, t + 1)
                sp.dma_start(ys_d[1 - shared][ds((t if shared else t - SHARED_TILES) * P, P), :], ob[:, k, :]
                             ).then_inc(ys_stored[k], 16)

            for k in range(XS_SLOTS):
                load(1, k, True)
            cuts = [0, shared_rounds - 2, shared_rounds, rounds - 3]
            for first, end in zip(cuts, cuts[1:]):
                if first == shared_rounds - 2:
                    sp.wait_ge(table_written, writes(BATCH))
                with sp.Fori(first, end) as i:
                    for k in range(XS_SLOTS):
                        load(i + 2, k, first < shared_rounds - 2)
                        store(i, k, first < shared_rounds)
            for t in range((rounds - 3) * XS_SLOTS, TILES):
                i, k = divmod(t, XS_SLOTS)
                if t + 2 * XS_SLOTS < TILES:
                    load(i + 2, k, False)
                store(i, k, False)
            for k in range(XS_SLOTS):
                sp.wait_ge(ys_stored[k], 16 * len(range(k, TILES, XS_SLOTS)))

        @block.gpsimd
        def _(pool):
            nc.gpsimd.memset(zeros[:, :], 0.0).then_inc(zeroed, 1)
            nc.gpsimd.memset(ident[:, :], 0.0).then_inc(setup, 1)
            nc.gpsimd.memset(below[:, :], 1.0).then_inc(setup, 1)
            nc.gpsimd.memset(before[:, :, :], 1.0).then_inc(setup, 1)
            nc.gpsimd.memset(ones[:, :], 1.0).then_inc(setup, 1)
            nc.gpsimd.iota(tile_i[:, :], pattern=[[1, SHARED_TILES]], base=0, channel_multiplier=0).then_inc(setup, 1)
            nc.gpsimd.iota(lane_i[:, :], pattern=[[1, 1]], base=0, channel_multiplier=1).then_inc(setup, 1)
            pool.wait_ge(setup, 6)
            nc.gpsimd.affine_select(out=ident[:, :], in_=ident[:, :], compare_op=ALU.not_equal, fill=1.0, base=0,
                                    pattern=[[-1, P]], channel_multiplier=1).then_inc(setup, 1)
            nc.gpsimd.affine_select(out=below[:, :], in_=below[:, :], compare_op=ALU.is_gt, fill=0.0, base=0,
                                    pattern=[[1, P]], channel_multiplier=-1).then_inc(setup, 1)
            nc.gpsimd.affine_select(out=before[:, :, :], in_=before[:, :, :], compare_op=ALU.is_gt, fill=0.0, base=0,
                                    pattern=[[1, EXPERTS], [-1, EXPERTS]], channel_multiplier=0).then_inc(setup, 1)

            def tail(gap, b):
                if gap == 23:
                    row = value(pool, b + 1)
                    pool.wait_ge(table_cleared, 16 * 2)
                    pool.wait_ge(pos_ready, row)
                    pool.wait_ge(read["rows"], row)
                if 23 <= gap < 23 + CH:
                    c = gap - 23
                    for j in range(TOPK):
                        i = j * CH + c
                        table_ = xs_d[int(isinstance(b, int) and b == BATCH - 1)]
                        nc.gpsimd.indirect_dma_start(table_, bass.IndirectOffsetOnAxis(ap=pos[:, i:i + 1], axis=0),
                                                     h2r[:, c, :], None).then_inc(table_written, 16)
                if gap == GAPS - 1:
                    if isinstance(b, int) and b == SHARED - 1:
                        pool.wait_ge(group, PAD_STEP)
                        for e in range(EXPERTS):
                            nc.gpsimd.indirect_dma_start(xs_d[0], bass.IndirectOffsetOnAxis(ap=pad[:, e:e + 1], axis=0),
                                                         zeros[:, :], None).then_inc(padded, 16)
                    pool.wait_ge(table_written, writes(b + 1))

            def scan(b, tail_b):
                for n in range(NSTATE):
                    step = b * NSTATE + n
                    if not on_dve(b, n):
                        pool.wait_ge(scanned, (step + 1) * HALVES)
                        pool.wait_ge(c_copied, (step + 1) * SEG)
                        nc.gpsimd.tensor_tensor(ring[:, n % RING], ring[:, n % RING],
                                                Csb[:, n % C_SLOTS, :].unsqueeze(1).to_broadcast([P, HALVES, SEQ]),
                                                ALU.mult).then_inc(prod_ready, 1)
                    for gap in (2 * n, 2 * n + 1):
                        if tail_b is not None:
                            tail(gap, tail_b)

            rows(lambda b: scan(b, None), lambda b: scan(b, b - 1), lambda b: scan(b, b - 1), pool)
            each_gap(BATCH - 1, tail)
            for b in range(BATCH):
                shared = b < SHARED
                if b in (0, SHARED):
                    for k in range(XS_SLOTS):
                        pool.wait_ge(ys_stored[k], 16 * len(range(k, SHARED_TILES if shared else TILES, XS_SLOTS)))
                    pool.wait_ge(group, GROUP_STEPS)
                    pool.wait_ge(rowstep, 1)
                for c in range(CH):
                    wait(pool, mixed, TOPK * (b * CH + c + 1 - GATH_SLOTS))
                    for j in range(TOPK):
                        i = (b * TOPK + j) * CH + c
                        nc.gpsimd.indirect_dma_start(gath[:, (b * CH + c) % GATH_SLOTS, j, :], None, ys_d[1 - shared],
                                                     bass.IndirectOffsetOnAxis(ap=pos_g[:, i:i + 1], axis=0)
                                                     ).then_inc(gathered[(b * CH + c) % GATH_SLOTS], 16)

        @block.tensor
        def _(pe):
            def product(out, lhsT, rhs, start=True, stop=True):
                return nc.tensor.matmul(out, lhsT, rhs, start=start, stop=stop)

            def turn(out, block_in, start=True):
                return nc.tensor.matmul(out, block_in, ident[0:block_in.shape[0], 0:block_in.shape[0]],
                                        is_transpose=True, start=start, stop=True, skip_group_check=True)

            before_fill = [None]

            def fill(name, b, work):
                if before_fill[0]:
                    pe.wait_ge(*before_fill[0])
                work().then_inc(filled[name], 1)
                before_fill[0] = (read[name], READS.get(name, 1) * (b + 1))

            def mean(b, k):
                def work():
                    for g in range(SEG):
                        last = product(PF[:, g * BANK:(g + 1) * BANK], mean_w[:, :], xT[:, ds(b * SEQ + g * BANK, BANK)])
                    return last
                fill(f"mean{k}", b, work)

            def var(b, k):
                pe.wait_ge(sq_ready[k], b + 1)

                def work():
                    for c in range(CH):
                        last = product(PF[:, c:c + 1], sq[:, c * P:(c + 1) * P], mean_w[:, 0:1])
                    return last
                fill(f"var{k}", b, work)

            def rstd(b, k):
                pe.wait_ge(rstd_ready[k], b + 1)

                def work():
                    for c in range(CH):
                        last = turn(PF[:, c * P:(c + 1) * P], small[:, 5, c:c + 1].to_broadcast([P, P]))
                    return last
                fill(f"rstd{k}", b, work)

            def from_h(name, b, w, a):
                def work():
                    for g in range(SEG):
                        last = product(PF[:, g * BANK:(g + 1) * BANK], w[:, a * P:(a + 1) * P],
                                       hT[:, g * BANK:(g + 1) * BANK])
                    return last
                fill(f"{name}{a}", b, work)

            def front(gap, b):
                if gap == 0:
                    if isinstance(b, int):
                        pe.wait_ge(loaded_x[b], 16)
                    else:
                        for row in range(BATCH):
                            pe.wait_ge(loaded_x[row], 16)
                    mean(b, 0)
                if gap == 3:
                    var(b, 0)
                if gap == 6:
                    rstd(b, 0)
                if gap == 8:
                    pe.wait_ge(h_ready[0], b + 1)
                if gap in (8, 10):
                    from_h("u", b, w1, gap // 2 - 4)
                if gap in (12, 14):
                    from_h("gate", b, w2, gap // 2 - 6)
                if gap == 19:
                    pe.wait_ge(u_ready, b + 1)

                    def work():
                        for g in range(SEG):
                            for a in range(HALVES):
                                last = product(PF[0:PROJ, g * BANK:(g + 1) * BANK], xproj[:, a, :],
                                               u[:, a, g * BANK:(g + 1) * BANK], a == 0, a == HALVES - 1)
                        return last
                    fill("xproj", b, work)
                if gap in (21, 23):
                    a = gap // 2 - 10

                    def work():
                        for g in range(SEG):
                            last = product(PF[:, g * BANK:(g + 1) * BANK], dtw[:, a * P:(a + 1) * P],
                                           xdt[:, g * BANK:(g + 1) * BANK])
                        return last
                    fill(f"dt{a}", b, work)

            def tail(gap, b):
                if gap in (4, 5):
                    a = gap - 4
                    pe.wait_ge(y_out, b + 1)

                    def work():
                        for c in range(CH):
                            last = turn(PF[:, c * P:(c + 1) * P], ysb[:, c, a * P:(a + 1) * P])
                        return last
                    fill(f"yT{a}", b, work)
                if gap == 9:
                    pe.wait_ge(read["yT1"], b + 1)

                    def work():
                        for g in range(SEG):
                            for a in range(HALVES):
                                last = product(PF[:, g * BANK:(g + 1) * BANK], wo[:, a, :],
                                               yg[:, a, g * BANK:(g + 1) * BANK], a == 0, a == HALVES - 1)
                        return last
                    fill("wo", b, work)
                if gap == 11:
                    pe.wait_ge(x1_ready, b + 1)
                    mean(b, 1)
                if gap == 13:
                    var(b, 1)
                if gap == 15:
                    rstd(b, 1)
                if gap == 17:
                    pe.wait_ge(h_ready[1], b + 1)

                    def work():
                        for c in range(CH):
                            last = product(PF[:, c * EXPERTS:(c + 1) * EXPERTS], hT[:, c * P:(c + 1) * P], router[:, :])
                        return last
                    fill("logit", b, work)
                if gap == 18:
                    def work():
                        for c in range(CH):
                            last = turn(PF[:, c * P:(c + 1) * P], hT[:, c * P:(c + 1) * P])
                        return last
                    fill("rows", b, work)
                if gap == 22:
                    pe.wait_ge(chosen_ready, b + 1)

                    def work():
                        product(PF[:, 0:RW], below[:, :], both[:, :])
                        return product(PF[:, BANK:BANK + RW], ones[:, :], both[:, :])
                    fill("prefix", b, work)

            def add_state(b, n):
                wait_product(pe, b, n)
                for c in range(CH):
                    for a in range(HALVES):
                        last = turn(PYc[:, c, a * P:(a + 1) * P], ring[:, n % RING, a, c * P:(c + 1) * P], start=False)
                last.then_inc(summed, 1)

            def start_y(b):
                wait(pe, y_out, b)
                for c in range(CH):
                    for a in range(HALVES):
                        nc.tensor.matmul(PYc[:, c, a * P:(a + 1) * P], u[:, a, c * P:(c + 1) * P], Ddiag[:, a, :],
                                         start=(c % 2 == 0 and a == 0), stop=True, skip_group_check=True)

            def fill_row(b, row, g, out, signal, done, count):
                last_read = value(pe, count)
                pe.wait_ge(mod_step, MOD_STEPS)
                wait(pe, done, last_read)
                product(out[g], pick[:, row:row + 1].to_broadcast([2 * 2 * NSTATE, P]),
                        bcs[:, ds(b % 2, 1), g * BANK:(g + 1) * BANK].squeeze(1)).then_inc(signal, 1)

            def fill_b(b, n):
                for g in range(SEG):
                    fill_row(b, n, g, PBC, b_filled, c_copied, (b * NSTATE + n - 1) * SEG + g + 1)

            def fill_c(b, n):
                for g in range(SEG):
                    fill_row(b, NSTATE + n, g, PBC, c_filled, dbu_ready, (b * NSTATE + n) * SEG + g + 1)

            def scan(b, tail_b, front_b):
                before_fill[0] = (read["dt1"], b + 1)
                for n in range(NSTATE):
                    fill_c(b, n)
                    gap_work(2 * n, tail_b, front_b)
                    if n + 1 < NSTATE:
                        fill_b(b, n + 1)
                    elif front_b is not None:
                        fill_b(front_b, 0)
                    if n == 2:
                        start_y(b)
                    elif n > 2:
                        for m in ((0, 1) if n == 3 else (n - 2,)):
                            add_state(b, m)
                    elif tail_b is not None:
                        add_state(b - 1, NSTATE - 2 + n)
                    gap_work(2 * n + 1, tail_b, front_b)

            def gap_work(gap, tail_b, front_b):
                if front_b is not None:
                    front(gap, front_b)
                if tail_b is not None:
                    tail(gap, tail_b)

            pe.wait_ge(loaded["c"], 48)
            pe.wait_ge(siluc_ready, 1)
            for k in range(6):
                last = product(PBC[0][:, k * BATCH:(k + 1) * BATCH], wmod[:, k, :], siluc[:, :])
            last.then_inc(mod_filled, 1)
            pe.wait_ge(setup, SETUP)
            pe.wait_ge(loaded["attn"], 16 * ATTN_LOADS)
            pe.wait_ge(mod_step, MOD_STEPS)
            each_gap(0, front)
            fill_b(0, 0)
            rows(lambda b: scan(b, None, b + 1), lambda b: scan(b, b - 1, b + 1), lambda b: scan(b, b - 1, None), pe)
            for n in (NSTATE - 2, NSTATE - 1):
                add_state(BATCH - 1, n)
            before_fill[0] = (read["prefix"], READS["prefix"] * (BATCH - 1))

            pe.wait_ge(loaded["gateup"], 32)
            pe.wait_ge(group, GROUP_STEPS)
            pe.wait_ge(y_out, BATCH)

            ahead = []
            held = [pe.alloc_register(f"held{k}") for k in range(XS_SLOTS)]

            def load_expert(k):
                return pe.value_load(expert[0:1, ds(k, 1)], min_val=0, max_val=EXPERTS - 1)

            def gate_up(k, par, e):
                pe.wait_ge(xt_read, k + 1)
                wait(pe, sg_ready, k - 1)
                product(PG(par)[:, 0:INTER], xsT[:, par % 2, :], gate_w[:, ds(e * INTER, INTER)]).then_inc(g_filled, 1)
                wait(pe, inner_ready, k)
                product(PU[:, 0:INTER], xsT[:, par % 2, :], up_w[:, ds(e * INTER, INTER)]).then_inc(u_filled, 1)

            def turn_inner(k, par):
                pe.wait_ge(inner_ready, k + 1)
                wait(pe, it_read, k)
                for c, (i0, w) in enumerate(INNER):
                    last = turn(PI[0:w, c * P:(c + 1) * P], inner[:, par % 2, i0:i0 + w])
                last.then_inc(it_filled, 1)

            def down(k, par, e):
                if isinstance(k, int) and k == 0:
                    pe.wait_ge(loaded["down"], 16 * NIN)
                pe.wait_ge(it_read, k + 1)
                wait(pe, o_read, k)
                for c, (i0, w) in enumerate(INNER):
                    last = product(PO, innerT[0:w, par % 2, c * P:(c + 1) * P],
                                   down_w[0:w, c, ds(e * HID, HID)], c == 0, c == NIN - 1)
                last.then_inc(o_filled, 1)

            def combine(m):
                h, rest = divmod(m, CH // SEG)
                if rest == 0 and 1 <= h <= BATCH * SEG:
                    h -= 1
                    wait(pe, mt_read, h)
                    pe.wait_ge(mixed, (h + 1) * (CH // SEG * TOPK))
                    for c in range(CH // SEG):
                        last = turn(PM[:, c * P:(c + 1) * P], mix[:, h % SEG * (CH // SEG) + c, :])
                    last.then_inc(mt_filled, 1)

            def tile(k, par, rnd):
                static = isinstance(k, int)
                if static and k == MIX_STEP // XS_SLOTS * XS_SLOTS:
                    pe.wait_ge(table, 3)
                if not static or k < TILES:
                    e_gate = ahead.pop() if ahead else load_expert(k)
                if not static or k + 1 < TILES:
                    slot = (par + 1) % XS_SLOTS
                    extra = 1 if par + 1 == XS_SLOTS else 0
                    pe.wait_ge(xs_loaded[slot], 16 * (rnd + extra + 1))
                    wait(pe, xt_read, k + 1)
                    turn(PX, xs[:, slot, :]).then_inc(xt_filled, 1)
                if not static or 0 <= k - 3 < TILES:
                    down(k - 3, par - 3, pe.snap(held[(par - 3) % XS_SLOTS], min_val=0, max_val=EXPERTS - 1))
                if not static or k < TILES:
                    gate_up(k, par, e_gate)
                    pe.reg_mov(held[par], e_gate)
                    if par < XS_SLOTS - 1 and not (static and k + 1 == TILES):
                        ahead.append(load_expert(k + 1))
                if not static or 0 <= k - 1 < TILES:
                    turn_inner(k - 1, par - 1)

            pe.wait_ge(xs_loaded[0], 16)
            turn(PX, xs[:, 0, :]).then_inc(xt_filled, 1)
            tile_schedule(pe, tile, tail, combine)

        @block.scalar
        def _(act):
            def square(b, k):
                act.wait_ge(read[f"mean{k}"], b + 1)
                nc.scalar.activation(sq, xc, ACT.Square).then_inc(sq_ready[k], 1)

            def rsqrt_seed(b, k):
                act.wait_ge(read[f"var{k}"], b + 1)
                nc.scalar.activation(small[:, 1, :], small[:, 0, :], ACT.Ln).then_inc(lnv_ready[k], 1)
                act.wait_ge(lnv_ready[k], b + 1)
                nc.scalar.activation(small[:, 2, :], small[:, 1, :], ACT.Exp, scale=-0.5).then_inc(y0_ready[k], 1)

            def modulate(b, k):
                count = value(act, b + 1)
                act.wait_ge(mod_step, MOD_STEPS)
                act.wait_ge(read[f"rstd{k}"], count)
                nc.scalar.activation(hT[:, :], xc, ACT.Identity, scale=mod[:, 3 * k + 1, ds(b, 1)],
                                     bias=mod[:, 3 * k, ds(b, 1)]).then_inc(h_ready[k], 1)

            def front(gap, b):
                par = b % 2
                if gap == 2:
                    square(b, 0)
                if gap == 4:
                    rsqrt_seed(b, 0)
                if gap == 7:
                    modulate(b, 0)
                if gap in (9, 11):
                    a = gap // 2 - 4
                    act.wait_ge(filled[f"u{a}"], b + 1)
                    nc.scalar.activation(ub[:, a, CONVK - 1:], PF, ACT.Identity, bias=cols[:, 0, a:a + 1]
                                         ).then_inc(read[f"u{a}"], 1)
                if gap in (11, 13):
                    a = gap // 2 - 5
                    act.wait_ge(pad_clear, b + 1)
                    act.wait_ge(read[f"u{a}"], b + 1)
                    wait(act, filled["wo"], b - 1)
                    nc.scalar.activation(z[:, a, :], ub[:, a, 0:SEQ], ACT.Identity, scale=conv[:, a, 0:1],
                                         bias=cols[:, 2, a:a + 1]).then_inc(conv_step[a], 1)
                if gap in (13, 15):
                    a = gap // 2 - 6
                    count = value(act, b + 1)
                    act.wait_ge(mod_step, MOD_STEPS)
                    act.wait_ge(filled[f"gate{a}"], count)
                    nc.scalar.activation(gate[:, ds(par, 1), a, :], PF.unsqueeze(1), ACT.Tanh, scale=0.5,
                                         bias=b2half[:, a:a + 1]).then_inc(read[f"gate{a}"], 1)
                if gap == 17:
                    for a in range(HALVES):
                        act.wait_ge(conv_step[a], (b + 1) * CONVK)
                    nc.scalar.activation(u[:, :, :], z[:, :, :], ACT.Tanh, scale=0.5).then_inc(tanhz_ready, 1)
                if gap == 18:
                    act.wait_ge(tanhz_ready, b + 1)
                    nc.scalar.activation(u[:, :, :], u[:, :, :], ACT.Identity, scale=0.5, bias=half[:, 0:1]
                                         ).then_inc(u_ready, 1)
                if gap == 20:
                    act.wait_ge(filled["xproj"], b + 1)
                    nc.scalar.copy(xdt[:, :], PF[0:DTRANK, :]).then_inc(read["xproj"], 1)
                if gap in (22, 24):
                    a = gap // 2 - 11
                    act.wait_ge(filled[f"dt{a}"], b + 1)
                    nc.scalar.activation(v_sb[:, a, :], PF, ACT.Identity, bias=cols[:, 3, a:a + 1]
                                         ).then_inc(read[f"dt{a}"], 1)
                if gap in (23, 25):
                    a = gap // 2 - 11
                    act.wait_ge(read[f"dt{a}"], b + 1)
                    nc.scalar.activation(e_sb[:, a, :], v_sb[:, a, :], ACT.Abs).then_inc(av_ready, 1)
                    act.wait_ge(av_ready, b * HALVES + a + 1)
                    nc.scalar.activation(e_sb[:, a, :], e_sb[:, a, :], ACT.Exp, scale=-1.0).then_inc(e_ready, 1)
                if gap in (24, 26):
                    a = gap // 2 - 12
                    act.wait_ge(e_ready, b * HALVES + a + 1)
                    nc.scalar.activation(w_sb[:, a, :], e_sb[:, a, :], ACT.Identity, bias=1.0).then_inc(w_ready, 1)
                if gap == 27:
                    for a in range(HALVES):
                        act.wait_ge(w_ready, b * HALVES + a + 1)
                        nc.scalar.activation(lw_sb[:, a, :], w_sb[:, a, :], ACT.Ln).then_inc(lw_ready, 1)

            def tail(gap, b):
                if gap == 3:
                    act.wait_ge(summed, NSTATE * (b + 1))
                    nc.scalar.copy(ysb[:, :, :].rearrange("p c m -> p (c m)"), PY).then_inc(y_out, 1)
                if gap == 9:
                    count = value(act, b + 1)
                    act.wait_ge(mod_step, MOD_STEPS)
                    act.wait_ge(filled["wo"], count)
                    nc.scalar.activation(o_sb, PF, ACT.Identity, scale=gahalf[:, ds(b, 1)], bias=gabo[:, ds(b, 1)]
                                         ).then_inc(read["wo"], 1)
                if gap == 12:
                    square(b, 1)
                if gap == 14:
                    rsqrt_seed(b, 1)
                if gap == 16:
                    modulate(b, 1)
                if gap == 18:
                    act.wait_ge(route, b * 12 + 2)
                    nc.scalar.activation(prob[:, :], prob[:, :], ACT.Exp).then_inc(prob_exp, 1)
                if gap == 19:
                    act.wait_ge(filled["rows"], b + 1)
                    act.wait_ge(table_cleared, 16 * 2)
                    scattered_before(act, b)
                    nc.scalar.copy(h2r[:, :, :].rearrange("p c h -> p (c h)"), PF).then_inc(read["rows"], 1)

            def gap_work(gap, tail_b, front_b):
                if front_b is not None:
                    front(gap, front_b)
                if tail_b is not None:
                    tail(gap, tail_b)

            def decays(b, n):
                for a in range(HALVES):
                    free = value(act, (b * NSTATE + n) * HALVES + a - DA_SLOTS + 1)
                    delta_count = value(act, b * HALVES + a + 1) if n == 0 else None
                    act.wait_ge(mod_step, MOD_STEPS)
                    if n == 0:
                        act.wait_ge(delta_ready, delta_count)
                    wait(act, scanned, free)
                    nc.scalar.activation(dA[:, (n * HALVES + a) % DA_SLOTS, :].unsqueeze(1),
                                         dd[:, ds(b % 2, 1), 0, a, :], ACT.Exp,
                                         scale=A[:, a, n:n + 1]).then_inc(da_ready, 1)

            def scan(b, tail_b, front_b):
                for n in range(NSTATE):
                    step = b * NSTATE + n
                    wait_product(act, b, n - C_SLOTS)
                    for g in range(SEG):
                        act.wait_ge(c_filled, step * SEG + g + 1)
                        nc.scalar.copy(Csb[:, n % C_SLOTS, g * BANK:(g + 1) * BANK], PBC[g]).then_inc(c_copied, 1)
                    gap_work(2 * n, tail_b, front_b)
                    if n + 1 < NSTATE:
                        decays(b, n + 1)
                    elif front_b is not None:
                        decays(front_b, 0)
                    gap_work(2 * n + 1, tail_b, front_b)

            act.wait_ge(loaded["c"], 48)
            nc.scalar.activation(siluc[:, :], cT[:, :], ACT.Silu).then_inc(siluc_ready, 1)
            act.wait_ge(loaded["attn"], 16 * ATTN_LOADS)
            nc.scalar.activation(A[:, :, :], A[:, :, :], ACT.Exp).then_inc(a_exp, 1)
            act.wait_ge(mod_step, MOD_STEPS)
            each_gap(0, front)
            decays(0, 0)
            rows(lambda b: scan(b, None, b + 1), lambda b: scan(b, b - 1, b + 1), lambda b: scan(b, b - 1, None), act)
            for gap in range(TAIL_GAP):
                tail(gap, BATCH - 1)

            def tile(k, par, rnd):
                static = isinstance(k, int)
                if not static or k < TILES:
                    act.wait_ge(g_filled, k + 1)
                    wait(act, sg_ready, k - 1)
                    nc.scalar.activation(th[:, par % 2, :], PG(par)[:, 0:INTER], ACT.Tanh, scale=0.5
                                         ).then_inc(tanh_ready, 1)
                if not static or 0 <= k - 1 < TILES:
                    act.wait_ge(it_filled, k)
                    wait(act, o_filled, k - 2)
                    nc.scalar.copy(innerT[:, (par - 1) % 2, :], PI[:, 0:NIN * P]).then_inc(it_read, 1)

            def combine(m):
                h, rest = divmod(m - 3, CH // SEG)
                if rest == 0 and 1 <= h <= BATCH * SEG:
                    act.wait_ge(mt_read, h)
                    cut = slice((h - 1) * BANK, h * BANK)
                    act.dma_start(outT_d[:, cut], xT[:, cut]).then_inc(stored, 16)

            tile_schedule(act, tile, tail, combine)
            act.wait_ge(stored, 16 * BATCH * SEG)

        @block.vector
        def _(dve):
            V = nc.vector

            def center(b, k):
                dve.wait_ge(filled[f"mean{k}"], b + 1)
                V.tensor_tensor(xc, xT[:, ds(b * SEQ, SEQ)], PF, ALU.subtract).then_inc(read[f"mean{k}"], 1)

            def variance(b, k):
                dve.wait_ge(filled[f"var{k}"], b + 1)
                V.tensor_scalar(small[:, 0, :], PF[:, 0:CH], LN_EPS, None, ALU.add).then_inc(read[f"var{k}"], 1)

            def rsqrt(b, k):
                dve.wait_ge(y0_ready[k], b + 1)
                V.tensor_tensor(small[:, 3, :], small[:, 0, :], small[:, 2, :], ALU.mult).then_inc(newton[k], 1)
                dve.wait_ge(newton[k], b * 3 + 1)
                V.tensor_tensor(small[:, 4, :], small[:, 3, :], small[:, 2, :], ALU.mult).then_inc(newton[k], 1)
                dve.wait_ge(newton[k], b * 3 + 2)
                V.tensor_scalar(small[:, 3, :], small[:, 4, :], -0.5, 1.5, ALU.mult, ALU.add).then_inc(newton[k], 1)
                dve.wait_ge(newton[k], b * 3 + 3)
                V.tensor_tensor(small[:, 5, :], small[:, 3, :], small[:, 2, :], ALU.mult).then_inc(rstd_ready[k], 1)

            def normalise(b, k):
                dve.wait_ge(filled[f"rstd{k}"], b + 1)
                V.tensor_tensor(xc, xc, PF, ALU.mult).then_inc(read[f"rstd{k}"], 1)

            def tap(b, a, k):
                dve.wait_ge(conv_step[a], b * CONVK + k)
                V.scalar_tensor_tensor(z[:, a, :], ub[:, a, k:k + SEQ], conv[:, a, k:k + 1], z[:, a, :],
                                       ALU.mult, ALU.add).then_inc(conv_step[a], 1)

            def front(gap, b):
                par = b % 2
                if gap == 2:
                    center(b, 0)
                if gap == 4:
                    variance(b, 0)
                if gap == 6:
                    rsqrt(b, 0)
                if gap == 7:
                    normalise(b, 0)
                if gap == 8:
                    V.memset(ubpad, 0.0).then_inc(pad_clear, 1)
                if gap == 13:
                    tap(b, 0, 1)
                    tap(b, 0, 2)
                if gap == 14:
                    tap(b, 1, 1)
                    tap(b, 0, 3)
                if gap in (15, 16):
                    tap(b, 1, gap - 13)
                if gap == 20:
                    rows_in = PF[DTRANK:PROJ, :].unsqueeze(1)
                    dve.wait_ge(filled["xproj"], b + 1)
                    V.tensor_copy(bcs[0:2 * NSTATE, ds(par, 1), :], rows_in).then_inc(read["xproj"], 1)
                    dve.wait_ge(read["xproj"], b * 3 + 2)
                    V.tensor_tensor(bcs[2 * NSTATE:4 * NSTATE, ds(par, 1), :], rows_in,
                                    bcs[0:2 * NSTATE, ds(par, 1), :].bitcast(fp32), ALU.subtract
                                    ).then_inc(read["xproj"], 1)
                half_of = {27: (lost, 0), 28: (lost, 1), 29: (log_part, 0), 30: (log_part, 1)}
                if gap in half_of:
                    work, a = half_of[gap]
                    work(b, a)
                if gap == 31:
                    dve.wait_ge(delta_ready, (b + 1) * HALVES)
                    for a in range(HALVES):
                        V.tensor_tensor(dd[:, ds(par, 1), 1, a, :], dd[:, ds(par, 1), 0, a, :], u[:, a, :].unsqueeze(1),
                                        ALU.mult).then_inc(du_ready, 1)

            def lost(b, a):
                count = b * HALVES + a + 1
                dve.wait_ge(w_ready, count)
                V.scalar_tensor_tensor(e_sb[:, a, :], w_sb[:, a, :], 1.0, e_sb[:, a, :], ALU.subtract, ALU.subtract
                                       ).then_inc(lost_ready, 1)
                dve.wait_ge(lost_ready, count)
                V.scalar_tensor_tensor(v_sb[:, a, :], v_sb[:, a, :], 0.0, e_sb[:, a, :], ALU.max, ALU.subtract
                                       ).then_inc(softplus_step, 1)

            def log_part(b, a):
                count = b * HALVES + a + 1
                dve.wait_ge(lw_ready, count)
                V.scalar_tensor_tensor(lw_sb[:, a, :], w_sb[:, a, :], 1.0, lw_sb[:, a, :], ALU.is_gt, ALU.mult
                                       ).then_inc(log_ready, 1)
                dve.wait_ge(softplus_step, count)
                dve.wait_ge(log_ready, count)
                V.tensor_tensor(dd[:, ds(b % 2, 1), 0, a, :], v_sb[:, a, :].unsqueeze(1), lw_sb[:, a, :].unsqueeze(1),
                                ALU.add).then_inc(delta_ready, 1)

            def per_chunk(v):
                return v.unsqueeze(2).to_broadcast([P, CH, EXPERTS])

            def by_expert(v, n=CH):
                return v.rearrange("p (c e) -> p c e", e=EXPERTS)

            def tail(gap, b):
                step = [b * 12]

                def then(ins):
                    ins.then_inc(route, 1)
                    step[0] = step[0] + 1
                    dve.wait_ge(route, step[0])

                if gap in (5, 6):
                    a = gap - 5
                    dve.wait_ge(filled[f"yT{a}"], b + 1)
                    V.scalar_tensor_tensor(yg[:, a, :].unsqueeze(1), gate[:, ds(b % 2, 1), a, :], 1.0, PF.unsqueeze(1),
                                           ALU.add, ALU.mult).then_inc(read[f"yT{a}"], 1)
                if gap == 11:
                    dve.wait_ge(read["wo"], b + 1)
                    V.tensor_tensor(xT[:, ds(b * SEQ, SEQ)], xT[:, ds(b * SEQ, SEQ)], o_sb, ALU.add).then_inc(x1_ready, 1)
                if gap == 12:
                    center(b, 1)
                if gap == 14:
                    variance(b, 1)
                if gap == 15:
                    rsqrt(b, 1)
                if gap == 16:
                    normalise(b, 1)
                if gap == 18:
                    dve.wait_ge(filled["logit"], b + 1)
                    then(V.tensor_copy(prob[:, :], PF[:, 0:RW]))
                    V.reduce_max(stat[:, 0, :], by_expert(prob[:, :]), AX.X).then_inc(read["logit"], 1)
                    dve.wait_ge(read["logit"], b + 1)
                    V.tensor_tensor(by_expert(prob[:, :]), by_expert(prob[:, :]), per_chunk(stat[:, 0, :]),
                                    ALU.subtract).then_inc(route, 1)
                if gap == 19:
                    step[0] = b * 12 + 2
                    dve.wait_ge(prob_exp, b + 1)
                    then(V.reduce_sum(stat[:, 0, :], by_expert(prob[:, :]), AX.X))
                    then(V.reciprocal(stat[:, 1, :], stat[:, 0, :]))
                    then(V.tensor_tensor(by_expert(prob[:, :]), by_expert(prob[:, :]), per_chunk(stat[:, 1, :]), ALU.mult))
                    shape = [P, CH, EXPERTS, EXPERTS]
                    p3 = by_expert(prob[:, :])
                    other, own = p3.unsqueeze(2).to_broadcast(shape), p3.unsqueeze(3).to_broadcast(shape)
                    ah, ti = (t[:, :].rearrange("p (c e f) -> p c e f", c=CH, e=EXPERTS) for t in (ahead, ties))
                    then(V.tensor_tensor(ti, other, own, ALU.is_equal))
                    then(V.tensor_tensor(ti, ti, before[:, :, :].unsqueeze(1).to_broadcast(shape), ALU.mult))
                    then(V.tensor_tensor(ah, other, own, ALU.is_gt))
                    then(V.tensor_tensor(ahead[:, :], ahead[:, :], ties[:, :], ALU.add))
                    then(V.reduce_sum(by_expert(rank[:, :]), ah, AX.X))
                    V.tensor_scalar(chosen[:, 0, :], rank[:, :], 0.0, None, ALU.is_equal).then_inc(route, 1)
                    V.tensor_scalar(chosen[:, 1, :], rank[:, :], 1.0, None, ALU.is_equal).then_inc(route, 1)
                    V.tensor_scalar(both[:, :], rank[:, :], TOPK - 0.5, None, ALU.is_lt).then_inc(chosen_ready, 1)
                if gap == 21:
                    dve.wait_ge(route, b * 12 + 12)
                    V.scalar_tensor_tensor(picked[:, :, :], chosen[:, :, :], 0.5,
                                           prob[:, :].unsqueeze(1).to_broadcast([P, TOPK, RW]), ALU.mult, ALU.mult
                                           ).then_inc(wsum, 1)
                    dve.wait_ge(wsum, b + 1)
                    V.reduce_sum(wsel[:, ds(b, 1), :].rearrange("p b (j c) -> p (b j) c", c=CH),
                                 picked[:, :, :].rearrange("p j (c e) -> p j c e", e=EXPERTS), AX.X).then_inc(wsel_ready, 1)
                if gap == 23:
                    positions(b)

            def tile_places(total, then):
                then(V.tensor_scalar(ntile_i[:, :], total, float(P - 1), None, ALU.add))
                then(V.tensor_scalar(ntile_i[:, :], ntile_i[:, :], P.bit_length() - 1, None, ALU.arith_shift_right))
                then(V.tensor_copy(ntile[:, :], ntile_i[:, :]))
                then(V.tensor_tensor(pairs8[:, :, :], before[:, :, :],
                                     ntile[:, :].unsqueeze(1).to_broadcast([P, EXPERTS, EXPERTS]), ALU.mult))
                then(V.reduce_sum(firsts[:, :], pairs8[:, :, :], AX.X))
                then(V.tensor_tensor(ends[:, :], firsts[:, :], ntile[:, :], ALU.add))

            def positions(b):
                last = isinstance(b, int) and b == BATCH - 1
                s = [b * 8]

                def then(ins):
                    ins.then_inc(place, 1)
                    s[0] = s[0] + 1
                    dve.wait_ge(place, s[0])

                dve.wait_ge(filled["prefix"], b + 1)
                V.tensor_copy(by_expert(slot_f[:, :]), by_expert(PF[:, 0:RW])).then_inc(read["prefix"], 1)
                V.tensor_copy(sums[:, 0, HEAD:, :], by_expert(PF[:, BANK:BANK + RW])).then_inc(read["prefix"], 1)
                dve.wait_ge(read["prefix"], 2 * (b + 1))
                for i, shift_ in enumerate((1, 2, 4)):
                    then(V.tensor_tensor(sums[:, (i + 1) % 2, HEAD:, :], sums[:, i % 2, HEAD:, :],
                                         sums[:, i % 2, HEAD - shift_:HEAD - shift_ + CH, :], ALU.add))
                total = sums[:, 1, HEAD + CH - 1, :]
                if last:
                    tile_places(total, then)
                    then(V.tensor_scalar(starts[:, :], firsts[:, :], float(P), None, ALU.mult))
                then(V.tensor_tensor(by_expert(slot_f[:, :]), by_expert(slot_f[:, :]),
                                     sums[:, 1, HEAD - 1:HEAD - 1 + CH, :], ALU.add))
                then(V.tensor_tensor(by_expert(slot_f[:, :]), by_expert(slot_f[:, :]),
                                     starts[:, :].unsqueeze(1).to_broadcast([P, CH, EXPERTS]), ALU.add))
                if not last:
                    then(V.tensor_tensor(starts[:, :], starts[:, :], total, ALU.add))
                then(V.tensor_tensor(picked[:, :, :], chosen[:, :, :],
                                     slot_f[:, :].unsqueeze(1).to_broadcast([P, TOPK, RW]), ALU.mult))
                then(V.reduce_sum(pos_f[:, :].rearrange("p (j c) -> p j c", j=TOPK),
                                  picked[:, :, :].rearrange("p j (c e) -> p j c e", e=EXPERTS), AX.X))
                scattered_before(dve, b)
                V.tensor_copy(pos[:, :], pos_f[:, :]).then_inc(pos_ready, 1)
                if last:
                    V.tensor_copy(pos_g[:, SHARED * TOPK * CH:], pos_f[:, :]).then_inc(rowstep, 1)
                    experts_of(SHARED_TILES, LAST_TILES, table, 0)
                else:
                    V.tensor_copy(pos_all[:, ds(b * (TOPK * CH), TOPK * CH)], pos_f[:, :]).then_inc(pos_kept, 1)
                if isinstance(b, int) and b == SHARED - 1:
                    shared_table()

            def experts_of(first, n, signal, count):
                shape = [P, n, EXPERTS]
                pt = past[:, 0:n * EXPERTS].rearrange("p (k e) -> p k e", e=EXPERTS)
                V.tensor_tensor(pt, tile_f[:, 0:n].unsqueeze(2).to_broadcast(shape),
                                ends[:, :].unsqueeze(1).to_broadcast(shape), ALU.is_ge).then_inc(signal, 1)
                dve.wait_ge(signal, count + 1)
                V.reduce_sum(expert_f[:, 0:n], pt, AX.X).then_inc(signal, 1)
                dve.wait_ge(signal, count + 2)
                V.tensor_scalar(expert[:, first:first + n], expert_f[:, 0:n], float(EXPERTS - 1), None, ALU.min
                                ).then_inc(signal, 1)
                return pt

            def shared_table():
                s = [0]

                def then(ins):
                    ins.then_inc(group, 1)
                    s[0] += 1
                    dve.wait_ge(group, s[0])

                then(V.tensor_scalar(pad[:, :], starts[:, :], lane_f[:, 0:1], None, ALU.add))
                then(V.tensor_tensor(free[:, :], starts[:, :], region_f[:, :], ALU.subtract))
                tile_places(free[:, :], then)
                then(V.tensor_scalar(free[:, :], ntile[:, :], float(-P), float(REGION), ALU.mult, ALU.add))
                pt = experts_of(0, SHARED_TILES, group, s[0])
                s[0] += 3
                dve.wait_ge(group, s[0])
                then(V.tensor_tensor(pt, pt, free[:, :].unsqueeze(1).to_broadcast([P, SHARED_TILES, EXPERTS]), ALU.mult))
                then(V.reduce_sum(expert_f[:, :], pt, AX.X))
                then(V.scalar_tensor_tensor(tile_row[:, :], tile_f[:, :], float(P), expert_f[:, :], ALU.mult, ALU.add))
                n = SHARED * TOPK * CH
                shape = [P, n, EXPERTS]
                sh = shift[:, :].rearrange("p (k e) -> p k e", e=EXPERTS)
                dve.wait_ge(pos_kept, SHARED)
                then(V.tensor_scalar(moved[:, :], pos_all[:, :], float(-REGION), None, ALU.add))
                then(V.tensor_tensor(sh, moved[:, :].unsqueeze(2).to_broadcast(shape),
                                     region_f[:, :].unsqueeze(1).to_broadcast(shape), ALU.is_ge))
                then(V.tensor_tensor(sh, sh, free[:, :].unsqueeze(1).to_broadcast(shape), ALU.mult))
                then(V.reduce_sum(moved[:, :], sh, AX.X))
                then(V.tensor_tensor(pos_g[:, 0:n], pos_all[:, :], moved[:, :], ALU.subtract))
                assert s[0] == GROUP_STEPS, s

            def gap_work(gap, tail_b, front_b):
                if front_b is not None:
                    front(gap, front_b)
                if tail_b is not None:
                    tail(gap, tail_b)

            def scan(b, tail_b, front_b):
                dve.wait_ge(du_ready, (b + 1) * HALVES)
                for n in range(NSTATE):
                    step = b * NSTATE + n
                    wait(dve, summed, step - RING + 1)
                    for g in range(SEG):
                        cut = slice(g * BANK, (g + 1) * BANK)
                        dve.wait_ge(b_filled, step * SEG + g + 1)
                        V.tensor_tensor(ring[:, n % RING, :, cut], dd[:, ds(b % 2, 1), 1, :, cut].squeeze(1),
                                        PBC[g].unsqueeze(1).to_broadcast([P, HALVES, BANK]), ALU.mult
                                        ).then_inc(dbu_ready, 1)
                    gap_work(2 * n, tail_b, front_b)
                    dve.wait_ge(dbu_ready, (step + 1) * SEG)
                    for a in range(HALVES):
                        dve.wait_ge(da_ready, step * HALVES + a + 1)
                        V.tensor_tensor_scan(ring[:, n % RING, a, :], dA[:, (n * HALVES + a) % DA_SLOTS, :],
                                             ring[:, n % RING, a, :], 0.0, ALU.mult, ALU.add).then_inc(scanned, 1)
                    if on_dve(b, n):
                        dve.wait_ge(scanned, (step + 1) * HALVES)
                        dve.wait_ge(c_copied, (step + 1) * SEG)
                        V.tensor_tensor(ring[:, n % RING], ring[:, n % RING],
                                        Csb[:, n % C_SLOTS, :].unsqueeze(1).to_broadcast([P, HALVES, SEQ]), ALU.mult
                                        ).then_inc(dve_prod_ready, 1)
                    gap_work(2 * n + 1, tail_b, front_b)

            V.memset(mean_w[:, :], 1.0 / HID).then_inc(mod_step, 1)
            V.memset(sums[:, :, :, :], 0.0).then_inc(mod_step, 1)
            V.memset(half[:, :], 0.5).then_inc(mod_step, 1)
            dve.wait_ge(setup, SETUP)
            V.tensor_tensor(pick[:, :], ident[0:4 * NSTATE, 0:2 * NSTATE], ident[0:4 * NSTATE, 2 * NSTATE:4 * NSTATE],
                            ALU.add).then_inc(mod_step, 1)
            V.tensor_copy(tile_f[:, :], tile_i[:, :]).then_inc(mod_step, 1)
            V.tensor_copy(lane_f[:, :], lane_i[:, :]).then_inc(mod_step, 1)
            V.tensor_scalar(region_f[:, :], tile_i[:, 0:EXPERTS], float(REGION), None, ALU.mult).then_inc(mod_step, 1)
            V.tensor_scalar(starts[:, :], tile_i[:, 0:EXPERTS], float(REGION), None, ALU.mult).then_inc(mod_step, 1)
            dve.wait_ge(mod_filled, 1)
            V.tensor_copy(mod[:, :, :], PBC[0][:, 0:6 * BATCH].rearrange("p (k b) -> p k b", k=6)).then_inc(mod_step, 1)
            dve.wait_ge(mod_step, 9)
            gates = mod[:, 2:6:3, :]
            V.tensor_scalar(modt[:, :, :], gates, -1.0, 0.25, ALU.mult, ALU.max).then_inc(mod_step, 1)
            dve.wait_ge(mod_step, 10)
            V.tensor_tensor(modt[:, :, :], modt[:, :, :], gates, ALU.max).then_inc(mod_step, 1)
            V.tensor_scalar(mod[:, 1:5:3, :], mod[:, 1:5:3, :], 1.0, None, ALU.add).then_inc(mod_step, 1)
            dve.wait_ge(mod_step, 12)
            V.tensor_scalar(gates, gates, 0.0, 2.0, ALU.is_ge, ALU.mult).then_inc(mod_step, 1)
            dve.wait_ge(mod_step, 13)
            V.scalar_tensor_tensor(gates, gates, -1.0, modt[:, :, :], ALU.add, ALU.mult).then_inc(mod_step, 1)
            dve.wait_ge(mod_step, 14)
            V.tensor_scalar(gabo[:, :], mod[:, 2, :], bo[:, 0:1], None, ALU.mult).then_inc(mod_step, 1)
            V.tensor_scalar(gahalf[:, :], mod[:, 2, :], 0.5, None, ALU.mult).then_inc(mod_step, 1)
            dve.wait_ge(loaded["attn"], 16 * ATTN_LOADS)
            for a in range(HALVES):
                V.tensor_scalar(Ddiag[:, a, :], ident[:, :], cols[:, 4, a:a + 1], None, ALU.mult).then_inc(mod_step, 1)
            V.tensor_scalar(b2half[:, :], cols[:, 1, :], 0.5, None, ALU.mult).then_inc(mod_step, 1)
            dve.wait_ge(a_exp, 1)
            V.tensor_scalar(A[:, :, :], A[:, :, :], -1.0, None, ALU.mult).then_inc(mod_step, 1)
            dve.wait_ge(mod_step, MOD_STEPS)

            each_gap(0, front)
            rows(lambda b: scan(b, None, b + 1), lambda b: scan(b, b - 1, b + 1), lambda b: scan(b, b - 1, None), dve)

            def turned(k, par):
                dve.wait_ge(xt_filled, k + 1)
                wait(dve, u_filled, k - 1)
                V.tensor_copy(xsT[:, par % 2, :], PX).then_inc(xt_read, 1)

            def tile(k, par, rnd):
                static = isinstance(k, int)
                if not static or k + 1 < TILES:
                    turned(k + 1, par + 1)
                if not static or 0 <= k - 3 < TILES:
                    slot = (par - 3) % XS_SLOTS
                    dve.wait_ge(o_filled, k - 2)
                    wait(dve, ys_stored[slot], 16 * (rnd + (-1 if par < 3 else 0)))
                    V.tensor_copy(ob[:, slot, :], PO).then_inc(o_read, 1)
                if not static or k < TILES:
                    dve.wait_ge(tanh_ready, k + 1)
                    wait(dve, inner_ready, k - 1)
                    V.scalar_tensor_tensor(sg[:, par % 2, :], th[:, par % 2, :], 1.0, PG(par)[:, 0:INTER], ALU.add, ALU.mult
                                           ).then_inc(sg_ready, 1)
                    dve.wait_ge(sg_ready, k + 1)
                    dve.wait_ge(u_filled, k + 1)
                    wait(dve, it_filled, k - 1)
                    V.tensor_tensor(inner[:, par % 2, :], sg[:, par % 2, :], PU[:, 0:INTER], ALU.mult).then_inc(inner_ready, 1)

            def combine(m):
                b, c = divmod(m, CH)
                if b < BATCH:
                    wait(dve, mt_filled, (m - CH) // (CH // SEG) + 1)
                    dve.wait_ge(gathered[m % GATH_SLOTS], 16 * TOPK * (m // GATH_SLOTS + 1))
                    V.tensor_scalar(mix[:, c, :], gath[:, m % GATH_SLOTS, 0, :], wsel[:, b, c:c + 1], None, ALU.mult
                                    ).then_inc(mixed, 1)
                    dve.wait_ge(mixed, 2 * m + 1)
                    V.scalar_tensor_tensor(mix[:, c, :], gath[:, m % GATH_SLOTS, 1, :], wsel[:, b, CH + c:CH + c + 1],
                                           mix[:, c, :], ALU.mult, ALU.add).then_inc(mixed, 1)
                h, rest = divmod(m - 1, CH // SEG)
                if rest == 0 and 1 <= h <= BATCH * SEG:
                    h -= 1
                    cut = slice(h * BANK, (h + 1) * BANK)
                    dve.wait_ge(mt_filled, h + 1)
                    V.scalar_tensor_tensor(xT[:, cut], PM, mod[:, 5, h // SEG:h // SEG + 1], xT[:, cut], ALU.mult, ALU.add
                                           ).then_inc(mt_read, 1)

            turned(0, 0)
            tile_schedule(dve, tile, tail, combine)


def kernel(**inputs):
    import numpy as np
    import concourse.bacc as bacc
    from concourse import mybir as mb
    from concourse.bass_utils import run_bass_kernel_spmd

    a = {k: np.asarray(v) for k, v in inputs.items()}
    at, ff = "L0_attn_", "L0_ffn_"
    columns = np.stack([a[at + k].reshape(HALVES, P) for k in ("b1", "b2", "conv_b", "dt_proj_b", "D_skip")])
    arrays = {
        "xT": a[at + "x"].reshape(NTOK, HID).T,
        "w1": a[at + "W1"], "w2": a[at + "W2"], "wo": a[at + "Wo"],
        "xproj": a[at + "x_proj_w"], "dtw": a[at + "dt_proj_w"], "alog": a[at + "A_log"], "conv": a[at + "conv_w"],
        "cols": columns.transpose(2, 0, 1).reshape(P, 5 * HALVES), "bo": a[at + "bo"].reshape(P, 1),
        "router": a[ff + "router_w"].T,
        "gate": a[ff + "gate_w"].reshape(EXPERTS * INTER, HID).T,
        "up": a[ff + "up_w"].reshape(EXPERTS * INTER, HID).T,
        "down": a[ff + "down_w"].transpose(0, 2, 1).reshape(EXPERTS * INTER, HID),
        "cT": a["L0_c"].T, "wmod": a["L0_wmod"],
    }
    arrays = {f"in_{k}": np.ascontiguousarray(v) for k, v in arrays.items()}
    nc = bacc.Bacc("TRN2", target_bir_lowering=False, num_devices=1)
    args = [nc.dram_tensor(k, v.shape, mb.dt.from_np(v.dtype), kind="ExternalInput").ap() for k, v in arrays.items()]
    out = nc.dram_tensor("out_T", (HID, NTOK), mb.dt.float32, kind="ExternalOutput").ap()
    token_tables, result_tables = (
        [nc.dram_tensor(f"{name}{k}", (n, HID), mb.dt.float32, kind="Internal").ap() for k, n in enumerate(sizes)]
        for name, sizes in (("token_table", (EXPERTS * REGION + SPARE_TILES * P, LAST_TILES * P)),
                            ("result_table", (SHARED_TILES * P, LAST_TILES * P))))
    adaln_kernel(nc, *args, out, token_tables, result_tables)
    r = run_bass_kernel_spmd(nc, [arrays], core_ids=[0])
    return np.ascontiguousarray(np.asarray(r.results[0]["out_T"]).T).reshape(BATCH, SEQ, HID)
```
